# Optimizing a Trainium2 kernel written in Bass

```python
import numpy as np
import jax
import jax.numpy as jnp

def _softmax(x, axis=-1):
    return jax.nn.softmax(x, axis=axis)

def _gelu(x):
    return jax.nn.gelu(x, approximate=True)

def _silu(x):
    return jax.nn.silu(x)

def _sigmoid(x):
    return jax.nn.sigmoid(x)

def _layernorm(x, axis=-1, eps=1e-05):
    m = jnp.mean(x, axis=axis, keepdims=True)
    v = jnp.var(x, axis=axis, keepdims=True)
    return (x - m) / jnp.sqrt(v + eps)

def _scatter_add(tgt, idx, src, axis=0):
    return tgt.at[idx].add(src)

def _segment_sum(src, seg, n):
    return jax.ops.segment_sum(src, seg, n)
kernel_name = 'mk_sandwich_d2_jaxref_r4_6a3e81'

def setup_inputs(seed: int=0):
    np.random.seed(seed)
    _w = jnp.asarray

    def _L0_attn_setup():
        import jax, jax.numpy as jnp
        import numpy as np
        import math
        N, S, E, H = (4, 1024, 256, 16)
        D = E // H
        key = jax.random.key(seed)
        ks = jax.random.split(key, 9)
        w = 1.0 / math.sqrt(E)
        mk = lambda k, shape: jax.random.normal(k, shape, jnp.float32) * w
        return {'x': jax.random.normal(ks[0], (N, S, E), jnp.float32), 'Wq': mk(ks[1], (E, E)), 'bq': mk(ks[2], (E,)), 'Wk': mk(ks[3], (E, E)), 'bk': mk(ks[4], (E,)), 'Wv': mk(ks[5], (E, E)), 'bv': mk(ks[6], (E,)), 'Wo': mk(ks[7], (E, E)), 'bo': mk(ks[8], (E,))}
    _L0_attn_in = _L0_attn_setup()

    def _L0_ffn_setup():
        import jax, jax.numpy as jnp
        import numpy as np
        E = 16
        G = 4
        EPG = E // G
        K = 4
        TOPK_GROUP = 2
        PER_GROUP_K = K // TOPK_GROUP

        def _route(xf, router_w, correction_bias):
            S = xf.shape[0]
            logits = xf @ router_w.T
            scores = jax.nn.sigmoid(logits)
            sb = scores + correction_bias
            grp_top = jax.lax.top_k(sb.reshape(S, G, EPG), PER_GROUP_K)[0]
            group_scores = grp_top.sum(axis=-1)
            _, group_idx = jax.lax.top_k(group_scores, TOPK_GROUP)
            group_mask = jnp.zeros((S, G), sb.dtype).at[jnp.arange(S)[:, None], group_idx].set(1.0)
            score_mask = jnp.broadcast_to(group_mask[:, :, None], (S, G, EPG)).reshape(S, E)
            masked = jnp.where(score_mask > 0, sb, -jnp.inf)
            _, topk_idx = jax.lax.top_k(masked, K)
            w = jnp.take_along_axis(scores, topk_idx, axis=1)
            w = w / (w.sum(axis=-1, keepdims=True) + 1e-20)
            return (topk_idx, w, scores)
        key = jax.random.key(seed)
        ks = jax.random.split(key, 9)
        B, T, C, H, HS = (2, 256, 256, 64, 512)
        std = 0.02
        return {'x': jax.random.normal(ks[0], (B, T, C), jnp.float32), 'router_w': jax.random.normal(ks[1], (E, C), jnp.float32) * std, 'correction_bias': jnp.zeros((E,), jnp.float32), 'gate_w': jax.random.normal(ks[2], (E, C, H), jnp.float32) * std, 'up_w': jax.random.normal(ks[3], (E, C, H), jnp.float32) * std, 'down_w': jax.random.normal(ks[4], (E, H, C), jnp.float32) * std, 'shared_gate_w': jax.random.normal(ks[5], (HS, C), jnp.float32) * std, 'shared_up_w': jax.random.normal(ks[6], (HS, C), jnp.float32) * std, 'shared_down_w': jax.random.normal(ks[7], (C, HS), jnp.float32) * std}
    _L0_ffn_in = _L0_ffn_setup()

    def _L1_attn_setup():
        import jax, jax.numpy as jnp
        from jax import lax
        import numpy as np
        D_MODEL = 256
        D_STATE = 16
        D_CONV = 4
        EXPAND = 2
        D_INNER = EXPAND * D_MODEL
        DT_RANK = D_MODEL // 16
        B, L = (1, 256)

        def _mamba(x, in_w, conv_w, conv_b, xproj_w, dt_w, dt_b, Alog, Dp, out_w):
            xz = x @ in_w.T
            xi, z = jnp.split(xz, 2, axis=-1)
            xc = lax.conv_general_dilated(jnp.swapaxes(xi, 1, 2), conv_w, (1,), [(D_CONV - 1, 0)], feature_group_count=D_INNER)
            u = jnp.swapaxes(jax.nn.silu(xc + conv_b[None, :, None]), 1, 2)
            x_dbl = u @ xproj_w.T
            dt = x_dbl[..., :DT_RANK]
            Bm = x_dbl[..., DT_RANK:DT_RANK + D_STATE]
            Cm = x_dbl[..., DT_RANK + D_STATE:]
            delta = jax.nn.softplus(dt @ dt_w.T + dt_b)
            A = -jnp.exp(Alog)
            dA = jnp.exp(jnp.einsum('bld,dn->bldn', delta, A))
            dBu = jnp.einsum('bld,bln,bld->bldn', delta, Bm, u)

            def step(h, inputs):
                a, b, c = inputs
                h = a * h + b
                return (h, jnp.einsum('bdn,bn->bd', h, c))
            h0 = jnp.zeros((x.shape[0], D_INNER, D_STATE), x.dtype)
            _, ys = lax.scan(step, h0, (jnp.moveaxis(dA, 1, 0), jnp.moveaxis(dBu, 1, 0), jnp.moveaxis(Cm, 1, 0)))
            y = jnp.moveaxis(ys, 0, 1) + u * Dp
            return y * jax.nn.silu(z) @ out_w.T

        def _block(x, fw_in_w, fw_conv_w, fw_conv_b, fw_xproj_w, fw_dt_w, fw_dt_b, fw_Alog, fw_Dp, fw_out_w, bw_in_w, bw_conv_w, bw_conv_b, bw_xproj_w, bw_dt_w, bw_dt_b, bw_Alog, bw_Dp, bw_out_w, proj_w, proj_b, ln_w, ln_b):
            out_fw = _mamba(x, fw_in_w, fw_conv_w, fw_conv_b, fw_xproj_w, fw_dt_w, fw_dt_b, fw_Alog, fw_Dp, fw_out_w) + x
            xb = jnp.flip(x, axis=1)
            out_bw = jnp.flip(_mamba(xb, bw_in_w, bw_conv_w, bw_conv_b, bw_xproj_w, bw_dt_w, bw_dt_b, bw_Alog, bw_Dp, bw_out_w) + xb, axis=1)
            out = jnp.concatenate([out_fw, out_bw], axis=-1) @ proj_w.T + proj_b
            mu = out.mean(-1, keepdims=True)
            var = out.var(-1, keepdims=True)
            return (out - mu) / jnp.sqrt(var + 1e-05) * ln_w + ln_b
        key = jax.random.key(seed)
        ks = jax.random.split(key, 8)

        def nrm(k, shape, s=0.02):
            return jax.random.normal(k, shape, jnp.float32) * s

        def mamba_params(kbase):
            k = jax.random.split(kbase, 7)
            return {'in_w': nrm(k[0], (2 * D_INNER, D_MODEL)), 'conv_w': nrm(k[1], (D_INNER, 1, D_CONV), 0.1), 'conv_b': nrm(k[2], (D_INNER,), 0.1), 'xproj_w': nrm(k[3], (DT_RANK + 2 * D_STATE, D_INNER)), 'dt_w': nrm(k[4], (D_INNER, DT_RANK), 0.1), 'dt_b': nrm(k[5], (D_INNER,), 0.1), 'Alog': jnp.log(jnp.broadcast_to(jnp.arange(1.0, D_STATE + 1, dtype=jnp.float32), (D_INNER, D_STATE))), 'Dp': jnp.ones((D_INNER,), jnp.float32), 'out_w': nrm(k[6], (D_MODEL, D_INNER))}
        fw = mamba_params(ks[0])
        bw = mamba_params(ks[1])
        inp = {'x': jax.random.normal(ks[2], (B, L, D_MODEL), jnp.float32)}
        for n, p in fw.items():
            inp['fw_' + n] = p
        for n, p in bw.items():
            inp['bw_' + n] = p
        inp['proj_w'] = nrm(ks[3], (D_MODEL, 2 * D_MODEL))
        inp['proj_b'] = jnp.zeros((D_MODEL,), jnp.float32)
        inp['ln_w'] = jnp.ones((D_MODEL,), jnp.float32)
        inp['ln_b'] = jnp.zeros((D_MODEL,), jnp.float32)
        return inp
    _L1_attn_in = _L1_attn_setup()

    def _L1_ffn_setup():
        import jax, jax.numpy as jnp
        import numpy as np

        def _bitlinear(x, w_latent):
            scale = jax.lax.stop_gradient(jnp.clip(jnp.mean(jnp.abs(w_latent), axis=1, keepdims=True), 1e-05, None))
            tern = jnp.clip(jnp.round(w_latent / scale), -1.0, 1.0)
            w = w_latent + jax.lax.stop_gradient(tern - w_latent)
            return x @ (w * scale).T
        key = jax.random.key(seed)
        ks = jax.random.split(key, 6)
        dim, hidden, rank = (256, 1024, 16)
        B, S = (4, 1024)
        x = jax.random.normal(ks[0], (B, S, dim), dtype=jnp.float32)
        w_fc = 0.02 * jax.random.normal(ks[1], (hidden, dim), dtype=jnp.float32)
        w_proj = 0.02 * jax.random.normal(ks[2], (dim, hidden), dtype=jnp.float32)
        u = 0.02 * jax.random.normal(ks[3], (hidden, rank), dtype=jnp.float32)
        v = 0.02 * jax.random.normal(ks[4], (rank, dim), dtype=jnp.float32)
        fast_b = jax.random.normal(ks[5], (rank, rank), dtype=jnp.float32)
        gate = jnp.float32(0.05)
        return {'x': x, 'fast_b': fast_b, 'w_fc': w_fc, 'w_proj': w_proj, 'u': u, 'v': v, 'gate': gate}
    _L1_ffn_in = _L1_ffn_setup()
    _d = {'L0_attn_x': _L0_attn_in['x'], 'L0_attn_Wq': _L0_attn_in['Wq'], 'L0_attn_bq': _L0_attn_in['bq'], 'L0_attn_Wk': _L0_attn_in['Wk'], 'L0_attn_bk': _L0_attn_in['bk'], 'L0_attn_Wv': _L0_attn_in['Wv'], 'L0_attn_bv': _L0_attn_in['bv'], 'L0_attn_Wo': _L0_attn_in['Wo'], 'L0_attn_bo': _L0_attn_in['bo'], 'L0_ffn_router_w': _L0_ffn_in['router_w'], 'L0_ffn_correction_bias': _L0_ffn_in['correction_bias'], 'L0_ffn_gate_w': _L0_ffn_in['gate_w'], 'L0_ffn_up_w': _L0_ffn_in['up_w'], 'L0_ffn_down_w': _L0_ffn_in['down_w'], 'L0_ffn_shared_gate_w': _L0_ffn_in['shared_gate_w'], 'L0_ffn_shared_up_w': _L0_ffn_in['shared_up_w'], 'L0_ffn_shared_down_w': _L0_ffn_in['shared_down_w'], 'L1_attn_fw_in_w': _L1_attn_in['fw_in_w'], 'L1_attn_fw_conv_w': _L1_attn_in['fw_conv_w'], 'L1_attn_fw_conv_b': _L1_attn_in['fw_conv_b'], 'L1_attn_fw_xproj_w': _L1_attn_in['fw_xproj_w'], 'L1_attn_fw_dt_w': _L1_attn_in['fw_dt_w'], 'L1_attn_fw_dt_b': _L1_attn_in['fw_dt_b'], 'L1_attn_fw_Alog': _L1_attn_in['fw_Alog'], 'L1_attn_fw_Dp': _L1_attn_in['fw_Dp'], 'L1_attn_fw_out_w': _L1_attn_in['fw_out_w'], 'L1_attn_bw_in_w': _L1_attn_in['bw_in_w'], 'L1_attn_bw_conv_w': _L1_attn_in['bw_conv_w'], 'L1_attn_bw_conv_b': _L1_attn_in['bw_conv_b'], 'L1_attn_bw_xproj_w': _L1_attn_in['bw_xproj_w'], 'L1_attn_bw_dt_w': _L1_attn_in['bw_dt_w'], 'L1_attn_bw_dt_b': _L1_attn_in['bw_dt_b'], 'L1_attn_bw_Alog': _L1_attn_in['bw_Alog'], 'L1_attn_bw_Dp': _L1_attn_in['bw_Dp'], 'L1_attn_bw_out_w': _L1_attn_in['bw_out_w'], 'L1_attn_proj_w': _L1_attn_in['proj_w'], 'L1_attn_proj_b': _L1_attn_in['proj_b'], 'L1_attn_ln_w': _L1_attn_in['ln_w'], 'L1_attn_ln_b': _L1_attn_in['ln_b'], 'L1_ffn_fast_b': _L1_ffn_in['fast_b'], 'L1_ffn_w_fc': _L1_ffn_in['w_fc'], 'L1_ffn_w_proj': _L1_ffn_in['w_proj'], 'L1_ffn_u': _L1_ffn_in['u'], 'L1_ffn_v': _L1_ffn_in['v'], 'L1_ffn_gate': _L1_ffn_in['gate']}
    _x0 = _d['L0_attn_x']
    _d['L0_attn_x'] = jax.random.normal(jax.random.fold_in(jax.random.key(seed), 1), (8, 1024, 256), dtype=_x0.dtype)
    del _x0
    return _d

def reference(L0_attn_x, L0_attn_Wq, L0_attn_bq, L0_attn_Wk, L0_attn_bk, L0_attn_Wv, L0_attn_bv, L0_attn_Wo, L0_attn_bo, L0_ffn_router_w, L0_ffn_correction_bias, L0_ffn_gate_w, L0_ffn_up_w, L0_ffn_down_w, L0_ffn_shared_gate_w, L0_ffn_shared_up_w, L0_ffn_shared_down_w, L1_attn_fw_in_w, L1_attn_fw_conv_w, L1_attn_fw_conv_b, L1_attn_fw_xproj_w, L1_attn_fw_dt_w, L1_attn_fw_dt_b, L1_attn_fw_Alog, L1_attn_fw_Dp, L1_attn_fw_out_w, L1_attn_bw_in_w, L1_attn_bw_conv_w, L1_attn_bw_conv_b, L1_attn_bw_xproj_w, L1_attn_bw_dt_w, L1_attn_bw_dt_b, L1_attn_bw_Alog, L1_attn_bw_Dp, L1_attn_bw_out_w, L1_attn_proj_w, L1_attn_proj_b, L1_attn_ln_w, L1_attn_ln_b, L1_ffn_fast_b, L1_ffn_w_fc, L1_ffn_w_proj, L1_ffn_u, L1_ffn_v, L1_ffn_gate):

    def _L0_attn_ref(x, Wq, bq, Wk, bk, Wv, bv, Wo, bo):
        import jax, jax.numpy as jnp
        import numpy as np
        import math
        N, S, E, H = (4, 1024, 256, 16)
        D = E // H
        n, s, e = x.shape
        h, d = (H, D)
        scale = 1.0 / math.sqrt(d)

        def proj(W, b):
            y = jnp.einsum('nse,fe->nsf', x, W) + b
            return y.reshape(n, s, h, d).transpose(0, 2, 1, 3)
        Q = proj(Wq, bq)
        K = proj(Wk, bk)
        V = proj(Wv, bv)
        scores = jnp.einsum('nqhd,nkhd->nhqk', Q, K) * scale
        attn = jax.nn.softmax(scores, axis=-1)
        out = jnp.einsum('nhql,nlhd->nqhd', attn, V)
        out = out.reshape(n, s, e)
        return jnp.einsum('nse,fe->nsf', out, Wo) + bo

    def _L0_ffn_ref(x, router_w, correction_bias, gate_w, up_w, down_w, shared_gate_w, shared_up_w, shared_down_w):
        import jax, jax.numpy as jnp
        import numpy as np
        E = 16
        G = 4
        EPG = E // G
        K = 4
        TOPK_GROUP = 2
        PER_GROUP_K = K // TOPK_GROUP

        def _route(xf, router_w, correction_bias):
            S = xf.shape[0]
            logits = xf @ router_w.T
            scores = jax.nn.sigmoid(logits)
            sb = scores + correction_bias
            grp_top = jax.lax.top_k(sb.reshape(S, G, EPG), PER_GROUP_K)[0]
            group_scores = grp_top.sum(axis=-1)
            _, group_idx = jax.lax.top_k(group_scores, TOPK_GROUP)
            group_mask = jnp.zeros((S, G), sb.dtype).at[jnp.arange(S)[:, None], group_idx].set(1.0)
            score_mask = jnp.broadcast_to(group_mask[:, :, None], (S, G, EPG)).reshape(S, E)
            masked = jnp.where(score_mask > 0, sb, -jnp.inf)
            _, topk_idx = jax.lax.top_k(masked, K)
            w = jnp.take_along_axis(scores, topk_idx, axis=1)
            w = w / (w.sum(axis=-1, keepdims=True) + 1e-20)
            return (topk_idx, w, scores)
        B, T, C = x.shape
        S = B * T
        xf = x.reshape(S, C)
        sg = xf @ shared_gate_w.T
        su = xf @ shared_up_w.T
        shared_out = jax.nn.silu(sg) * su @ shared_down_w.T
        topk_idx, w, _scores = _route(xf, router_w, correction_bias)
        combine = jnp.zeros((S, E), xf.dtype).at[jnp.arange(S)[:, None], topk_idx].add(w)
        g = jnp.einsum('sc,ech->esh', xf, gate_w)
        u = jnp.einsum('sc,ech->esh', xf, up_w)
        h = jax.nn.silu(g) * u
        hw = h * combine.T[:, :, None]
        routed = jnp.einsum('esh,ehc->sc', hw, down_w)
        return (shared_out + routed).reshape(B, T, C)

    def _L1_attn_ref(x, fw_in_w, fw_conv_w, fw_conv_b, fw_xproj_w, fw_dt_w, fw_dt_b, fw_Alog, fw_Dp, fw_out_w, bw_in_w, bw_conv_w, bw_conv_b, bw_xproj_w, bw_dt_w, bw_dt_b, bw_Alog, bw_Dp, bw_out_w, proj_w, proj_b, ln_w, ln_b):
        import jax, jax.numpy as jnp
        from jax import lax
        import numpy as np
        D_MODEL = 256
        D_STATE = 16
        D_CONV = 4
        EXPAND = 2
        D_INNER = EXPAND * D_MODEL
        DT_RANK = D_MODEL // 16
        B, L = (1, 256)

        def _mamba(x, in_w, conv_w, conv_b, xproj_w, dt_w, dt_b, Alog, Dp, out_w):
            xz = x @ in_w.T
            xi, z = jnp.split(xz, 2, axis=-1)
            xc = lax.conv_general_dilated(jnp.swapaxes(xi, 1, 2), conv_w, (1,), [(D_CONV - 1, 0)], feature_group_count=D_INNER)
            u = jnp.swapaxes(jax.nn.silu(xc + conv_b[None, :, None]), 1, 2)
            x_dbl = u @ xproj_w.T
            dt = x_dbl[..., :DT_RANK]
            Bm = x_dbl[..., DT_RANK:DT_RANK + D_STATE]
            Cm = x_dbl[..., DT_RANK + D_STATE:]
            delta = jax.nn.softplus(dt @ dt_w.T + dt_b)
            A = -jnp.exp(Alog)
            dA = jnp.exp(jnp.einsum('bld,dn->bldn', delta, A))
            dBu = jnp.einsum('bld,bln,bld->bldn', delta, Bm, u)

            def step(h, inputs):
                a, b, c = inputs
                h = a * h + b
                return (h, jnp.einsum('bdn,bn->bd', h, c))
            h0 = jnp.zeros((x.shape[0], D_INNER, D_STATE), x.dtype)
            _, ys = lax.scan(step, h0, (jnp.moveaxis(dA, 1, 0), jnp.moveaxis(dBu, 1, 0), jnp.moveaxis(Cm, 1, 0)))
            y = jnp.moveaxis(ys, 0, 1) + u * Dp
            return y * jax.nn.silu(z) @ out_w.T

        def _block(x, fw_in_w, fw_conv_w, fw_conv_b, fw_xproj_w, fw_dt_w, fw_dt_b, fw_Alog, fw_Dp, fw_out_w, bw_in_w, bw_conv_w, bw_conv_b, bw_xproj_w, bw_dt_w, bw_dt_b, bw_Alog, bw_Dp, bw_out_w, proj_w, proj_b, ln_w, ln_b):
            out_fw = _mamba(x, fw_in_w, fw_conv_w, fw_conv_b, fw_xproj_w, fw_dt_w, fw_dt_b, fw_Alog, fw_Dp, fw_out_w) + x
            xb = jnp.flip(x, axis=1)
            out_bw = jnp.flip(_mamba(xb, bw_in_w, bw_conv_w, bw_conv_b, bw_xproj_w, bw_dt_w, bw_dt_b, bw_Alog, bw_Dp, bw_out_w) + xb, axis=1)
            out = jnp.concatenate([out_fw, out_bw], axis=-1) @ proj_w.T + proj_b
            mu = out.mean(-1, keepdims=True)
            var = out.var(-1, keepdims=True)
            return (out - mu) / jnp.sqrt(var + 1e-05) * ln_w + ln_b
        return _block(x, fw_in_w, fw_conv_w, fw_conv_b, fw_xproj_w, fw_dt_w, fw_dt_b, fw_Alog, fw_Dp, fw_out_w, bw_in_w, bw_conv_w, bw_conv_b, bw_xproj_w, bw_dt_w, bw_dt_b, bw_Alog, bw_Dp, bw_out_w, proj_w, proj_b, ln_w, ln_b)

    def _L1_ffn_ref(x, fast_b, w_fc, w_proj, u, v, gate):
        import jax, jax.numpy as jnp
        import numpy as np

        def _bitlinear(x, w_latent):
            scale = jax.lax.stop_gradient(jnp.clip(jnp.mean(jnp.abs(w_latent), axis=1, keepdims=True), 1e-05, None))
            tern = jnp.clip(jnp.round(w_latent / scale), -1.0, 1.0)
            w = w_latent + jax.lax.stop_gradient(tern - w_latent)
            return x @ (w * scale).T
        h = _bitlinear(x, w_fc) + gate * (x @ v.T @ fast_b.T @ u.T)
        r = jnp.maximum(h, 0.0)
        return _bitlinear(r * r, w_proj)
    x = L0_attn_x
    x = x + _layernorm(_L0_attn_ref(_layernorm(x, axis=-1), L0_attn_Wq, L0_attn_bq, L0_attn_Wk, L0_attn_bk, L0_attn_Wv, L0_attn_bv, L0_attn_Wo, L0_attn_bo), axis=-1)
    x = x + _layernorm(_L0_ffn_ref(_layernorm(x, axis=-1), L0_ffn_router_w, L0_ffn_correction_bias, L0_ffn_gate_w, L0_ffn_up_w, L0_ffn_down_w, L0_ffn_shared_gate_w, L0_ffn_shared_up_w, L0_ffn_shared_down_w), axis=-1)
    x = x + _layernorm(_L1_attn_ref(_layernorm(x, axis=-1), L1_attn_fw_in_w, L1_attn_fw_conv_w, L1_attn_fw_conv_b, L1_attn_fw_xproj_w, L1_attn_fw_dt_w, L1_attn_fw_dt_b, L1_attn_fw_Alog, L1_attn_fw_Dp, L1_attn_fw_out_w, L1_attn_bw_in_w, L1_attn_bw_conv_w, L1_attn_bw_conv_b, L1_attn_bw_xproj_w, L1_attn_bw_dt_w, L1_attn_bw_dt_b, L1_attn_bw_Alog, L1_attn_bw_Dp, L1_attn_bw_out_w, L1_attn_proj_w, L1_attn_proj_b, L1_attn_ln_w, L1_attn_ln_b), axis=-1)
    x = x + _layernorm(_L1_ffn_ref(_layernorm(x, axis=-1), L1_ffn_fast_b, L1_ffn_w_fc, L1_ffn_w_proj, L1_ffn_u, L1_ffn_v, L1_ffn_gate), axis=-1)
    return x

_drawn_inputs = setup_inputs


def setup_inputs(seed=0):
    import zlib

    import numpy as np

    out = dict(_drawn_inputs(seed))
    spreads = {'L0_ffn_correction_bias': (0.0, 0.1),
     'L1_attn_fw_Dp': (1.0, 0.6),
     'L1_attn_bw_Dp': (1.0, 0.6),
     'L1_attn_proj_b': (0.0, 0.8),
     'L1_attn_ln_w': (1.0, 0.2),
     'L1_attn_ln_b': (0.0, 0.1)}
    factors = {'L1_attn_fw_in_w': 8.0,
     'L1_attn_fw_conv_w': 8.0,
     'L1_attn_fw_conv_b': 8.0,
     'L1_attn_fw_xproj_w': 8.0,
     'L1_attn_fw_dt_w': 8.0,
     'L1_attn_fw_dt_b': 22.093,
     'L1_attn_fw_Alog': 8.0,
     'L1_attn_fw_out_w': 8.0,
     'L1_attn_bw_in_w': 8.0,
     'L1_attn_bw_conv_w': 8.0,
     'L1_attn_bw_conv_b': 8.0,
     'L1_attn_bw_xproj_w': 8.0,
     'L1_attn_bw_dt_w': 8.0,
     'L1_attn_bw_dt_b': 8.0,
     'L1_attn_bw_Alog': 8.0,
     'L1_attn_bw_out_w': 8.0,
     'L1_ffn_fast_b': 4.433,
     'L1_ffn_u': 4.435,
     'L1_ffn_v': 4.401}
    for name, (base, spread) in spreads.items():
        noise = np.random.default_rng([zlib.crc32(name.encode()), seed]).standard_normal(out[name].shape)
        drawn = base * np.exp(spread * noise) if base else spread * noise
        out[name] = jnp.asarray(drawn.astype(out[name].dtype))
    for name, factor in factors.items():
        out[name] = (out[name] * factor).astype(out[name].dtype)
    return out
```

```python
from contextlib import ExitStack

import concourse.bass as bass
import numpy as np
from concourse import mybir

F32 = mybir.dt.float32
BF16 = mybir.dt.bfloat16
ALU = mybir.AluOpType
ACT = mybir.ActivationFunctionType
AX = mybir.AxisListType

P = 128
NSEQ, T, C = 8, 1024, 256
KC = C // P
NT = T // P
CH = 512
NCH = T // CH
H, D = 16, 16
NE, HE = 16, 64
NG, PG = 4, 4
TOPK, TOPG = 4, 2
HS = 512
NJ = (NE * HE + HS) // P
DI, DS, DTR, TAPS = 512, 16, 16, 4
NDI = DI // P
XP = DTR + 2 * DS
HF, RANK = 1024, 16
NF = HF // P
EPS = 1e-5
ROUND = 12582912.0
BIG = 3.0e38


def col(ap):
    return ap.rearrange("p (a t) -> p a t", a=1)


class Phase:

    def __init__(self, nc, names):
        self.nc, self.names = nc, names.split()

    def __enter__(self):
        self.stack = ExitStack()
        self.sems = [self.stack.enter_context(self.nc.semaphore(n)) for n in self.names]
        self.block = self.stack.enter_context(self.nc.Block())
        return self.block, self.sems

    def __exit__(self, *failed):
        self.stack.close()
        nums = [s.num for s in self.sems]
        if not failed[0]:
            self.nc.all_engine_barrier(sems_to_clear=range(min(nums), max(nums) + 1))


def build(nc, a, out):
    ctx = ExitStack()
    with ctx:
        def sb(name, shape, dt=F32):
            return ctx.enter_context(nc.sbuf_tensor(name, shape, dt))

        xt = sb("xt", [P, NT, C])
        xnT = sb("xnT", [P, KC, T])
        ytok = sb("ytok", [P, NT, C])
        ident = sb("ident", [P, P])
        inT = sb("inT", [P, 2, KC, 2 * DI])
        xpT = sb("xpT", [P, 2, NDI, XP])
        dtT = sb("dtT", [DTR, 2, DI])
        WcT = sb("WcT", [P, 2, NDI, C])
        PxT = sb("PxT", [P, KC, C])
        WfT = sb("WfT", [P, KC, HF])
        WpT = sb("WpT", [P, NF, C])
        bo = sb("bo", [P, C])
        pb = sb("pb", [P, C])
        lnw = sb("lnw", [P, C])
        lnb = sb("lnb", [P, C])
        rwT = sb("rwT", [P, KC, NE])
        cbias = sb("cbias", [P, NE])
        tri = sb("tri", [P, NE, NE])
        ones = sb("ones", [1, P])
        mx = sb("mx", [P, 2, H])
        es = sb("es", [P, 2, H])
        convw = sb("convw", [P, 2, NDI, TAPS])
        convb = sb("convb", [P, 2, NDI])
        dtb = sb("dtb", [P, 2, NDI])
        Dp = sb("Dp", [P, 2, NDI])
        Aneg = sb("Aneg", [P, 2, NDI, DS])
        half = sb("half", [P, NT])
        st = sb("st", [P, NT, 6])
        mv = sb("mv", [P, NT, 2])
        rstd = sb("rstd", [P, NT])
        gatec = sb("gatec", [P, 1])
        KB = 256
        WORK = 126 * KB
        wk = sb("wk", [P, WORK])
        ps = ctx.enter_context(nc.psum_tensor("ps", [P, 8 * CH], F32))

        def area(at, *shape, dt=F32):
            n = int(np.prod(shape)) // (2 if dt == BF16 else 1)
            assert at + n <= WORK, (at, shape)
            v = wk[:, at:at + n]
            v = v if dt == F32 else v.bitcast(dt)
            names = "abcd"[:len(shape)]
            if len(shape) == 1:
                return v
            return v.rearrange("p (%s) -> p %s" % (" ".join(names), " ".join(names)),
                               **{k: s for k, s in zip(names, shape)})

        def bank(i, n=1):
            return ps[:, i * CH:(i + n) * CH]

        prodS = [area((24 + 16 * i) * KB, D, H * H) for i in range(2)]
        prodO = [area((56 + 16 * i) * KB, H, D, H) for i in range(2)]
        qs, ks, vs, Es = [[area((88 + 2 * n + i) * KB, D, H) for i in range(2)] for n in range(4)]
        brow = area(96 * KB, 3 * C)[0:1, :]
        On = [area((124 + i) * KB, C) for i in range(2)]
        An = area(24 * KB, NT, C)
        AnT = area(32 * KB, KC, T)
        wqkT = area(116 * KB, KC, 2 * C)
        wvT = area(120 * KB, KC, C)
        woT = area(122 * KB, KC, C)
        wgT = area(0, KC, NJ * P)
        wuT = area(12 * KB, KC, NJ * P)
        wdn = area(104 * KB, NJ, C)
        sel = area(99 * KB, NE // 2, P)
        hid = area(32 * KB, NCH, NJ, CH)
        sil = area(80 * KB, 2, CH)
        combT = area(84 * KB, T)
        route = area(88 * KB, 11 * KB)
        u_ = [area((8 * i) * KB, NDI, CH) for i in range(2)]
        sz = [area((16 + 8 * i) * KB, NDI, CH) for i in range(2)]
        dl = [area((32 + 8 * i) * KB, NDI, CH) for i in range(2)]
        XW = CH + TAPS
        du = [area(48 * KB + i * NDI * XW, NDI, XW) for i in range(2)]
        at = 48 * KB + 2 * NDI * XW
        hb = [area(at + 8 * KB * i, NDI, CH) for i in range(3)]
        at += 24 * KB
        dA = [area(at + 8 * KB * i, NDI, CH) for i in range(2)]
        at += 16 * KB
        Bb = [area(at + 2 * KB * i, CH) for i in range(2)]
        Cb = [area(at + 4 * KB + 2 * KB * i, CH) for i in range(2)]
        at += 8 * KB
        xd = area(at, CH)
        tl = [area(at + 2 * KB + 2 * KB * i, CH) for i in range(2)]
        tt = [area(at + 6 * KB + 2 * KB * i, CH) for i in range(2)]
        at += 10 * KB
        carry = area(at, DS, NDI)
        halo = area(at + DS * NDI, NDI, TAPS - 1)
        r2 = [area(16 * KB * i, NF, CH) for i in range(2)]
        rl = area(32 * KB, 2, CH)

        o_scr = nc.dram_tensor("o_scr", (H, T, D), F32, kind="Internal").ap()
        bc_scr = nc.dram_tensor("bc_scr", (2, 2 * DS, CH), F32, kind="Internal").ap()

        wl = area(0, NF, C)
        wp = area(8 * KB, KC, HF)
        ow = area(16 * KB, 2, KC, DI)
        pr = area(24 * KB, 2, KC, C)
        uT = area(28 * KB, HF)
        vv = area(32 * KB, C)
        fbt = area(33 * KB, RANK)
        Yr = area(34 * KB, HF)
        sc = area(38 * KB, NF + KC)
        rc = area(38 * KB + 16, NF + KC)
        q_ = area(40 * KB, NF, C)
        qp_ = area(48 * KB, KC, HF)
        alog = area(56 * KB, 2, NDI, DS)
        with Phase(nc, "loaded halved made scaled ternary bit_t bit_c low_mm low_ev comb_mm comb_ev") as (block, sems):
            loaded, halved, made, scaled, ternary, bit_t, bit_c, low_mm, low_ev, comb_mm, comb_ev = sems
            LOADS = [(ident[:], a["ident"]), (tri[:].rearrange("p a b -> p (a b)"), a["tri"]),
                     (inT[:], a["inT"]), (xpT[:], a["xpT"]), (dtT[:], a["dtT"]), (rwT[:], a["rwT"]),
                     (convw[:], a["convw"]), (convb[:], a["convb"]), (dtb[:], a["dtb"]), (Dp[:], a["Dp"]),
                     (wl, a["wfc"]), (wp, a["wproj"]), (ow, a["outw"]), (pr, a["projT"]),
                     (uT[0:RANK, :], a["uT"]), (vv[0:RANK, :], a["v"]), (fbt[0:RANK, :], a["fastb"]),
                     (alog, a["alog"]),
                     (wqkT, a["wqkT"]), (wvT, a["wvT"]), (woT, a["woT"])]
            ROWS = [(bo, "bo"), (pb, "projb"), (lnw, "lnw"), (lnb, "lnb"), (cbias, "cbias"),
                    (gatec, "gate")]
            NLOAD = 16 * (len(LOADS) + len(ROWS))

            @block.sync
            def _(sp):
                for dst, src in LOADS:
                    sp.dma_start(dst, src).then_inc(loaded, 16)
                for dst, name in ROWS:
                    src = a[name]
                    sp.dma_start(dst[:], src.broadcast_to([P, src.shape[1]])).then_inc(loaded, 16)
                sp.wait_ge(loaded, NLOAD)

            @block.gpsimd
            def _(pool):
                nc.gpsimd.memset(half[:], -0.5).then_inc(halved, 1)
                pool.wait_ge(halved, 1)

            @block.scalar
            def _(act):
                act.wait_ge(loaded, NLOAD)
                nc.scalar.activation(Aneg[:], alog, ACT.Exp).then_inc(low_ev, 1)
                act.wait_ge(low_mm, 2)
                nc.scalar.copy(Yr[0:RANK, :], bank(6, 2)[0:RANK, :]).then_inc(low_ev, 1)
                for d in range(2):
                    act.wait_ge(comb_mm, d + 1)
                    nc.scalar.copy(WcT[:, d, :, :].rearrange("p a b -> p (a b)"), bank(4, 2)).then_inc(comb_ev, 1)
                for n in range(2):
                    act.wait_ge(bit_t, n + 1)
                    dst = WfT[:].rearrange("p a b -> p (a b)") if n == 0 else WpT[:].rearrange("p a b -> p (a b)")
                    nc.scalar.copy(dst, bank(0, 4)).then_inc(bit_c, 1)

            @block.vector
            def _(dve):
                dve.wait_ge(loaded, NLOAD)
                nc.vector.memset(ones[:], 1.0).then_inc(made, 1)
                nc.vector.tensor_tensor(PxT[:], pr[:, 0, :, :], pr[:, 1, :, :], ALU.add).then_inc(made, 1)
                dve.wait_ge(low_ev, 1)
                nc.vector.tensor_scalar(Aneg[:], Aneg[:], -1.0, None, ALU.mult).then_inc(made, 1)
                nc.vector.tensor_reduce(sc[:, 0:NF], wl, AX.X, ALU.add, apply_absolute_value=True).then_inc(scaled, 1)
                nc.vector.tensor_reduce(sc[:, NF:], wp, AX.X, ALU.add, apply_absolute_value=True).then_inc(scaled, 1)
                dve.wait_ge(scaled, 2)
                nc.vector.tensor_scalar(sc[:, 0:NF], sc[:, 0:NF], 1.0 / C, 1e-5, ALU.mult, ALU.max).then_inc(scaled, 1)
                nc.vector.tensor_scalar(sc[:, NF:], sc[:, NF:], 1.0 / HF, 1e-5, ALU.mult, ALU.max).then_inc(scaled, 1)
                dve.wait_ge(scaled, 4)
                nc.vector.reciprocal(rc, sc).then_inc(scaled, 1)
                dve.wait_ge(scaled, 5)
                rows = [(wl[:, j, :], q_[:, j, :], j) for j in range(NF)]
                rows += [(wp[:, j, :], qp_[:, j, :], NF + j) for j in range(KC)]
                n = 0
                for w, q, j in rows:
                    nc.vector.tensor_scalar(q, w, rc[:, j:j + 1], ROUND, ALU.mult, ALU.add).then_inc(ternary, 1)
                for w, q, j in rows:
                    dve.wait_ge(ternary, n + len(rows))
                    n += 1
                    nc.vector.tensor_scalar(q, q, -ROUND, 1.0, ALU.add, ALU.min).then_inc(ternary, 1)
                dve.wait_ge(ternary, 2 * len(rows))
                for w, q, j in rows:
                    nc.vector.scalar_tensor_tensor(out=q, in0=q, scalar=-1.0, in1=w, op0=ALU.max,
                                                   op1=ALU.subtract).then_inc(ternary, 1)
                dve.wait_ge(ternary, 3 * len(rows))
                for w, q, j in rows:
                    nc.vector.tensor_tensor(q, q, w, ALU.add).then_inc(ternary, 1)
                dve.wait_ge(ternary, 4 * len(rows))
                for w, q, j in rows:
                    nc.vector.tensor_scalar(q, q, sc[:, j:j + 1], None, ALU.mult).then_inc(ternary, 1)
                for k in range(KC):
                    dve.wait_ge(low_mm, 2 + 2 * (k + 1))
                    dve.wait_ge(bit_c, 1)
                    for c in range(2):
                        w = WfT[:, k, c * CH:(c + 1) * CH]
                        nc.vector.scalar_tensor_tensor(out=w, in0=bank(6 + c), scalar=gatec[:, 0:1], in1=w,
                                                       op0=ALU.mult, op1=ALU.add).then_inc(made, 1)

            @block.tensor
            def _(pe):
                pe.wait_ge(loaded, NLOAD)
                for c in range(2):
                    nc.tensor.matmul(bank(6 + c)[0:RANK, :], fbt[0:RANK, :], uT[0:RANK, c * CH:(c + 1) * CH],
                                     start=True, stop=True).then_inc(low_mm, 1)
                for d in range(2):
                    if d:
                        pe.wait_ge(comb_ev, d)
                    for e in range(NDI):
                        for k in range(KC):
                            mm = nc.tensor.matmul(bank(4, 2)[:, e * C:(e + 1) * C], ow[:, d, k, e * P:(e + 1) * P],
                                                  pr[:, d, k, :], start=(k == 0), stop=(k == KC - 1))
                    mm.then_inc(comb_mm, 1)
                nrow = NF + KC
                pe.wait_ge(ternary, 5 * nrow)
                for k in range(KC):
                    for j in range(NF):
                        mm = nc.tensor.transpose(ps[:, (k * NF + j) * P:(k * NF + j + 1) * P],
                                                 q_[:, j, k * P:(k + 1) * P], ident[:])
                mm.then_inc(bit_t, 1)
                pe.wait_ge(bit_c, 1)
                for j in range(NF):
                    for k in range(KC):
                        mm = nc.tensor.transpose(ps[:, (j * KC + k) * P:(j * KC + k + 1) * P],
                                                 qp_[:, k, j * P:(j + 1) * P], ident[:])
                mm.then_inc(bit_t, 1)
                pe.wait_ge(low_ev, 2)
                for k in range(KC):
                    if k:
                        pe.wait_ge(made, 3 + 2 * k)
                    for c in range(2):
                        nc.tensor.matmul(bank(6 + c), vv[0:RANK, k * P:(k + 1) * P],
                                         Yr[0:RANK, c * CH:(c + 1) * CH], start=True, stop=True).then_inc(low_mm, 1)

        def ln_vector(dve, src, dst, nth, stat, aggr, rs_done, applied):
            for i in range(NT):
                nc.vector.bn_stats(st[:, i, :], src[:, i, :]).then_inc(stat, 1)
            for i in range(NT):
                dve.wait_ge(stat, nth * NT + i + 1)
                nc.vector.bn_aggr(mv[:, i, :], st[:, i, :]).then_inc(aggr, 1)
            dve.wait_ge(aggr, (nth + 1) * NT)
            dve.wait_ge(rs_done, 2 * (nth + 1))
            for i in range(NT):
                nc.vector.tensor_scalar(dst[:, i, :], src[:, i, :], mv[:, i, 0:1], rstd[:, i:i + 1],
                                        ALU.subtract, ALU.mult).then_inc(applied, 1)

        def ln_pool(pool, nth, aggr, rs_done):
            pool.wait_ge(aggr, (nth + 1) * NT)
            nc.gpsimd.tensor_scalar(rstd[:], mv[:, :, 1], EPS, None, ALU.add).then_inc(rs_done, 1)
            pool.wait_ge(rs_done, 2 * nth + 1)
            nc.gpsimd.tensor_tensor(rstd[:], rstd[:], half[:], ALU.pow).then_inc(rs_done, 1)

        def xn_tensor(pe, applied, base, xn_t):
            for i in range(NT):
                pe.wait_ge(applied, base + i + 1)
                for k in range(KC):
                    mm = nc.tensor.transpose(ps[:, k * T + i * P:k * T + (i + 1) * P],
                                             ytok[:, i, k * P:(k + 1) * P], ident[:])
                if i % 4 == 3:
                    mm.then_inc(xn_t, 1)

        def xn_scalar(act, xn_t, xn_ready, nth=0):
            for c in range(NCH):
                act.wait_ge(xn_t, nth * NCH + c + 1)
                for k in range(KC):
                    nc.scalar.copy(xnT[:, k, c * CH:(c + 1) * CH], bank(2 * k + c)).then_inc(xn_ready, 1)

        CLOSE = " stat aggr rs_done applied added xn_t xn_ready"

        def close_vector(dve, s, inner=False, last=False, first=0):
            stat, aggr, rs_done, applied, added = s[:5]
            n = first
            if inner:
                ln_vector(dve, ytok, ytok, n, stat, aggr, rs_done, applied)
                n = 1
                for i in range(NT):
                    dve.wait_ge(applied, i + 1)
                    nc.vector.tensor_tensor(ytok[:, i, :], ytok[:, i, :], lnw[:], ALU.mult).then_inc(applied, 1)
                for i in range(NT):
                    dve.wait_ge(applied, NT + i + 1)
                    nc.vector.tensor_tensor(ytok[:, i, :], ytok[:, i, :], lnb[:], ALU.add).then_inc(applied, 1)
                dve.wait_ge(applied, 3 * NT)
            ln_vector(dve, ytok, ytok, n, stat, aggr, rs_done, applied)
            if not last:
                dve.wait_ge(added, NT)
                ln_vector(dve, xt, ytok, n + 1, stat, aggr, rs_done, applied)

        def close_pool(pool, s, inner=False, last=False, first=0):
            stat, aggr, rs_done, applied, added = s[:5]
            n = first
            if inner:
                ln_pool(pool, 0, aggr, rs_done)
                n = 1
            ln_pool(pool, n, aggr, rs_done)
            base = 3 * NT if inner else first * NT
            for i in range(NT):
                pool.wait_ge(applied, base + i + 1)
                nc.gpsimd.tensor_tensor(xt[:, i, :], xt[:, i, :], ytok[:, i, :], ALU.add).then_inc(added, 1)
            if not last:
                ln_pool(pool, n + 1, aggr, rs_done)

        with nc.Fori(0, NSEQ) as seq:
            with Phase(nc, "x_in brow_in moe_in qk_mm v_mm q_ev k_ev v_ev qk_prod s_sum mx_made s_sub exp_done es_made "
                       "rs_made pv_prod pv_sum o_made o_out0 o_out1 an_in an_t ant_ev wo_mm wo_ev" + CLOSE) as (block, sems):
                (x_in, brow_in, moe_in, qk_mm, v_mm, q_ev, k_ev, v_ev, qk_prod, s_sum, mx_made, s_sub, exp_done, es_made,
                 rs_made, pv_prod, pv_sum, o_made, o_out0, o_out1, an_in, an_t, ant_ev, wo_mm, wo_ev, *cs) = sems
                stat, aggr, rs_done, applied, added, xn_t, xn_ready = cs
                o_out = (o_out0, o_out1)

                @block.sync
                def _(sp):
                    sp.dma_start(xt[:], a["x"].rearrange("s (i p) c -> (s i) p c", p=P)[bass.ds(seq * NT, NT), :, :]
                                 .rearrange("i p c -> p i c"))\
                        .then_inc(x_in, 16)
                    sp.dma_start(brow, a["brow"]).then_inc(brow_in, 16)
                    sp.dma_start(wgT, a["wgT"]).then_inc(moe_in, 16)
                    sp.dma_start(wuT, a["wuT"]).then_inc(moe_in, 16)
                    sp.dma_start(wdn, a["wdn"]).then_inc(moe_in, 16)
                    sp.dma_start(sel[0:NE, :, :], a["sel"]).then_inc(moe_in, 16)
                    for i in range(NT):
                        sp.wait_ge(o_made, i + 1)
                        sp.dma_start(o_scr[:, i * P:(i + 1) * P, :].rearrange("q t d -> t q d"),
                                     On[i % 2].rearrange("p (q d) -> p q d", d=D)).then_inc(o_out[i % 2], 16)
                    for j in range(2):
                        sp.wait_ge(o_out[j], 16 * (NT // 2))
                    rows = o_scr.rearrange("q (s u) d -> (q s) (u d)", u=C // D)
                    for i in range(NT):
                        if i:
                            sp.wait_ge(an_in, 16 * i)
                        sp.dma_start(An[:, i, :], rows[i * P:(i + 1) * P, :]).then_inc(an_in, 16)
                    sp.wait_ge(an_in, 16 * NT)
                    sp.wait_ge(moe_in, 64)

                @block.tensor
                def _(pe):
                    def project(i):
                        if i >= 2:
                            pe.wait_ge(q_ev, i - 1)
                            pe.wait_ge(k_ev, i - 1)
                            pe.wait_ge(v_ev, i - 1)
                        for k in range(KC):
                            nc.tensor.matmul(bank(4 + i % 2), xnT[:, k, i * P:(i + 1) * P], wqkT[:, k, :],
                                             start=(k == 0), stop=False)
                        nc.tensor.matmul(bank(4 + i % 2), ones[0:1, :], brow[:, 0:2 * C], start=False, stop=True)\
                            .then_inc(qk_mm, 1)
                        for k in range(KC):
                            nc.tensor.matmul(bank(6 + i % 2)[:, 0:C], xnT[:, k, i * P:(i + 1) * P], wvT[:, k, :],
                                             start=(k == 0), stop=False)
                        nc.tensor.matmul(bank(6 + i % 2)[:, 0:C], ones[0:1, :], brow[:, 2 * C:], start=False,
                                         stop=True).then_inc(v_mm, 1)

                    xn_tensor(pe, applied, 0, xn_t)
                    pe.wait_ge(brow_in, 16)
                    pe.wait_ge(xn_ready, 2 * NCH)
                    project(0)
                    project(1)
                    for i in range(NT):
                        pe.wait_ge(qk_prod, i + 1)
                        if i >= 2:
                            pe.wait_ge(s_sub, i - 1)
                        for d in range(D):
                            mm = nc.tensor.matmul(bank(i % 2)[:, 0:H * H], ident[:], prodS[i % 2][:, d, :],
                                                  start=(d == 0), stop=(d == D - 1))
                        mm.then_inc(s_sum, 1)
                        if i + 2 < NT:
                            project(i + 2)
                    for i in range(NT):
                        pe.wait_ge(an_in, 16 * (i + 1))
                        if i == 0:
                            pe.wait_ge(q_ev, NT)
                            pe.wait_ge(k_ev, NT)
                            pe.wait_ge(s_sub, NT)
                            pe.wait_ge(v_ev, NT)
                        if i >= 2:
                            pe.wait_ge(ant_ev, i - 1)
                        for k in range(KC):
                            mm = nc.tensor.transpose(bank(2 + i % 2)[:, k * P:(k + 1) * P], An[:, i, k * P:(k + 1) * P],
                                                     ident[:])
                        mm.then_inc(an_t, 1)
                    for i in range(NT):
                        pe.wait_ge(ant_ev, i + 1)
                        if i >= 2:
                            pe.wait_ge(wo_ev, i - 1)
                        for k in range(KC):
                            mm = nc.tensor.matmul(bank(6 + i % 2)[:, 0:C], AnT[:, k, i * P:(i + 1) * P], woT[:, k, :],
                                                  start=(k == 0), stop=(k == KC - 1))
                        mm.then_inc(wo_mm, 1)
                    xn_tensor(pe, applied, 2 * NT, xn_t)

                @block.scalar
                def _(act):
                    def by_feature(ap):
                        return ap.rearrange("p (h d) -> p d h", d=D)

                    def spread(i):
                        act.wait_ge(qk_mm, i + 1)
                        if i >= 2:
                            act.wait_ge(qk_prod, i - 1)
                            act.wait_ge(pv_prod, i - 1)
                        nc.scalar.activation(qs[i % 2], by_feature(bank(4 + i % 2)[:, 0:C]), ACT.Copy, scale=0.25)\
                            .then_inc(q_ev, 1)
                        nc.scalar.copy(ks[i % 2], by_feature(bank(4 + i % 2)[:, C:2 * C])).then_inc(k_ev, 1)
                        act.wait_ge(v_mm, i + 1)
                        nc.scalar.copy(vs[i % 2], by_feature(bank(6 + i % 2)[:, 0:C])).then_inc(v_ev, 1)

                    xn_scalar(act, xn_t, xn_ready)
                    spread(0)
                    spread(1)
                    for i in range(NT):
                        act.wait_ge(s_sub, i + 1)
                        e = Es[i % 2].rearrange("p a b -> p (a b)")
                        nc.scalar.activation(e, e, ACT.Exp).then_inc(exp_done, 1)
                        if i + 2 < NT:
                            spread(i + 2)
                    for i in range(NT):
                        act.wait_ge(an_t, i + 1)
                        nc.scalar.copy(AnT[:, :, i * P:(i + 1) * P],
                                       bank(2 + i % 2)[:, 0:C].rearrange("p (k t) -> p k t", k=KC)).then_inc(ant_ev, 1)
                    xn_scalar(act, xn_t, xn_ready, 1)

                @block.vector
                def _(dve):
                    def products(i):
                        dve.wait_ge(q_ev, i + 1)
                        dve.wait_ge(k_ev, i + 1)
                        if i >= 2:
                            dve.wait_ge(s_sum, i - 1)
                        nc.vector.tensor_tensor(
                            prodS[i % 2].rearrange("p d (q k) -> p d q k", k=H),
                            qs[i % 2].rearrange("p d (q a) -> p d q a", a=1).broadcast_to([P, D, H, H]),
                            ks[i % 2].rearrange("p d (a k) -> p d a k", a=1).broadcast_to([P, D, H, H]),
                            ALU.mult).then_inc(qk_prod, 1)

                    def maxima(i):
                        s = bank(i % 2)[:, 0:H * H].rearrange("p (q k) -> p q k", k=H)
                        dve.wait_ge(s_sum, i + 1)
                        nc.vector.reduce_max(mx[:, i % 2, :], s, AX.X).then_inc(mx_made, 1)
                        dve.wait_ge(mx_made, i + 1)
                        if i >= 2:
                            dve.wait_ge(pv_prod, i - 1)
                            dve.wait_ge(es_made, i - 1)
                        nc.vector.tensor_tensor(Es[i % 2], s, mx[:, i % 2, :].rearrange("p (q a) -> p q a", a=1)
                                                .broadcast_to([P, H, H]), ALU.subtract).then_inc(s_sub, 1)

                    def outputs(i):
                        dve.wait_ge(exp_done, i + 1)
                        nc.vector.reduce_sum(es[:, i % 2, :], Es[i % 2], AX.X).then_inc(es_made, 1)
                        dve.wait_ge(pv_prod, i + 1)
                        if i >= 2:
                            dve.wait_ge(o_out[i % 2], 16 * (i // 2))
                        nc.vector.tensor_reduce(On[i % 2], prodO[i % 2].rearrange("p q d k -> p (q d) k"), AX.X,
                                                ALU.add).then_inc(pv_sum, 1)
                        dve.wait_ge(es_made, i + 1)
                        nc.vector.reciprocal(es[:, i % 2, :], es[:, i % 2, :]).then_inc(rs_made, 1)
                        dve.wait_ge(pv_sum, i + 1)
                        dve.wait_ge(rs_made, i + 1)
                        o = On[i % 2].rearrange("p (q d) -> p q d", d=D)
                        nc.vector.tensor_tensor(o, o, es[:, i % 2, :].rearrange("p (q a) -> p q a", a=1)
                                                .broadcast_to([P, H, D]), ALU.mult).then_inc(o_made, 1)

                    dve.wait_ge(x_in, 16)
                    ln_vector(dve, xt, ytok, 0, stat, aggr, rs_done, applied)
                    products(0)
                    for i in range(NT):
                        if i + 1 < NT:
                            products(i + 1)
                        maxima(i)
                        if i:
                            outputs(i - 1)
                    outputs(NT - 1)
                    for i in range(NT):
                        dve.wait_ge(wo_mm, i + 1)
                        nc.vector.tensor_tensor(ytok[:, i, :], bank(6 + i % 2)[:, 0:C], bo[:], ALU.add)\
                            .then_inc(wo_ev, 1)
                    dve.wait_ge(wo_ev, NT)
                    close_vector(dve, cs, first=1)

                @block.gpsimd
                def _(pool):
                    ln_pool(pool, 0, aggr, rs_done)
                    for i in range(NT):
                        pool.wait_ge(exp_done, i + 1)
                        pool.wait_ge(v_ev, i + 1)
                        if i >= 2:
                            pool.wait_ge(pv_sum, i - 1)
                        nc.gpsimd.tensor_tensor(
                            prodO[i % 2],
                            Es[i % 2].rearrange("p q (a k) -> p q a k", a=1).broadcast_to([P, H, D, H]),
                            vs[i % 2].rearrange("p (a d) k -> p a d k", a=1).broadcast_to([P, H, D, H]),
                            ALU.mult).then_inc(pv_prod, 1)
                    close_pool(pool, cs, first=1)

            ORDER = list(range(NE // 2, NJ)) + list(range(NE // 2))
            with Phase(nc, "lg_mm lg_exp rt comb_t comb_ev g_mm u_mm c_mm sil_done h_made hc_made y_mm y_ev"
                       + CLOSE) as (block, sems):
                lg_mm, lg_exp, rt, comb_t, comb_ev, g_mm, u_mm, c_mm, sil_done, h_made, hc_made, y_mm, y_ev, *cs = sems
                stat, aggr, rs_done, applied, added, xn_t, xn_ready = cs
                NS = NCH * NJ

                W = NT * NE
                off = [0]
                routed = []

                def rtile(*shape):
                    n = int(np.prod(shape))
                    v = route[:, off[0]:off[0] + n]
                    off[0] += n
                    names = "abcd"[:len(shape)]
                    return v.rearrange("p (%s) -> p %s" % (" ".join(names), " ".join(names)),
                                       **{k: z for k, z in zip(names, shape)}) if len(shape) > 1 else v

                sg = rtile(NT, NE)
                sbv = rtile(NT * NG, PG)
                hi = rtile(NT * NG, 2)
                lo = rtile(NT * NG, 2)
                gs = rtile(NT, NG)
                g2 = rtile(NT * NG)
                gcmp = rtile(NT * NG * NG)
                geq = rtile(NT * NG * NG)
                grank = rtile(NT * NG)
                comb = rtile(NT, NE)
                wsum = rtile(NT)

                NQ = NT // 2
                ecmp = rtile(NQ, NE * NE)
                @block.vector
                def _(dve):
                    n = [0]

                    def link(ins):
                        n[0] += 1
                        ins.then_inc(rt, 1)

                    def settle():
                        dve.wait_ge(rt, n[0])

                    V = nc.vector
                    sgf = sg.rearrange("p a b -> p (a b)")
                    sbf = sbv.rearrange("p a b -> p (a b)")
                    dve.wait_ge(lg_exp, 1)
                    link(V.tensor_scalar(sgf, sgf, 1.0, None, ALU.add)); settle()
                    link(V.reciprocal(sgf, sgf)); settle()
                    link(V.tensor_tensor(sbf.rearrange("p (a b) -> p a b", b=NE), sg,
                                         col(cbias[:]).broadcast_to([P, NT, NE]), ALU.add)); settle()
                    link(V.tensor_tensor(hi, sbv[:, :, 0:2], sbv[:, :, 2:4], ALU.max))
                    link(V.tensor_tensor(lo, sbv[:, :, 0:2], sbv[:, :, 2:4], ALU.min)); settle()
                    link(V.tensor_tensor(g2, hi[:, :, 0], hi[:, :, 1], ALU.min))
                    link(V.tensor_tensor(hi[:, :, 0], hi[:, :, 0], hi[:, :, 1], ALU.max))
                    link(V.tensor_tensor(lo[:, :, 0], lo[:, :, 0], lo[:, :, 1], ALU.max)); settle()
                    link(V.tensor_tensor(g2, g2, lo[:, :, 0], ALU.max)); settle()
                    link(V.tensor_tensor(gs.rearrange("p a b -> p (a b)"), hi[:, :, 0], g2, ALU.add)); settle()
                    for i in range(NT):
                        o = gcmp[:, i * NG * NG:(i + 1) * NG * NG].rearrange("p (a b) -> p a b", a=NG)
                        e = geq[:, i * NG * NG:(i + 1) * NG * NG].rearrange("p (a b) -> p a b", a=NG)
                        other = col(gs[:, i, :]).broadcast_to([P, NG, NG])
                        own = gs[:, i, :].rearrange("p (a b) -> p a b", b=1).broadcast_to([P, NG, NG])
                        link(V.tensor_tensor(o, other, own, ALU.is_gt))
                        link(V.tensor_tensor(e, other, own, ALU.is_equal))
                    settle()
                    e4 = geq.rearrange("p (i a b) -> p i a b", a=NG, b=NG)
                    for i in range(NT):
                        link(V.tensor_tensor(e4[:, i, :, :], e4[:, i, :, :], tri[:, 0:NG, 0:NG], ALU.mult))
                    settle()
                    link(V.tensor_tensor(gcmp, gcmp, geq, ALU.add)); settle()
                    link(V.tensor_reduce(grank, gcmp.rearrange("p (g b) -> p g b", b=NG), AX.X, ALU.add)); settle()
                    link(V.tensor_scalar(grank, grank, float(TOPG), None, ALU.is_lt)); settle()
                    mask = grank.rearrange("p (g a) -> p g a", a=1).broadcast_to([P, NT * NG, PG])
                    link(V.tensor_tensor(sbv, sbv, mask, ALU.mult))
                    link(V.tensor_scalar(g2, grank, BIG, -BIG, ALU.mult, ALU.add)); settle()
                    link(V.tensor_tensor(sbv, sbv, g2.rearrange("p (g a) -> p g a", a=1)
                                         .broadcast_to([P, NT * NG, PG]), ALU.add)); settle()
                    eq_ = hid[:, 1, 0:2, :].rearrange("p a b -> p (a b)")
                    combf = comb.rearrange("p a b -> p (a b)")
                    for q in range(NT // NQ):
                        for i in range(NQ):
                            m = sbf[:, (q * NQ + i) * NE:(q * NQ + i + 1) * NE]
                            other = col(m).broadcast_to([P, NE, NE])
                            own = m.rearrange("p (a b) -> p a b", b=1).broadcast_to([P, NE, NE])
                            link(V.tensor_tensor(ecmp[:, i, :].rearrange("p (a b) -> p a b", a=NE), other, own, ALU.is_gt))
                            link(V.tensor_tensor(eq_[:, i * NE * NE:(i + 1) * NE * NE]
                                                 .rearrange("p (a b) -> p a b", a=NE), other, own, ALU.is_equal))
                        settle()
                        eqs = eq_[:, 0:NQ * NE * NE].rearrange("p (i a) -> p i a", i=NQ)
                        link(V.tensor_tensor(eqs, eqs, col(tri[:].rearrange("p a b -> p (a b)"))
                                             .broadcast_to([P, NQ, NE * NE]), ALU.mult)); settle()
                        link(V.tensor_tensor(ecmp, ecmp, eqs, ALU.add)); settle()
                        link(V.tensor_reduce(combf[:, q * NQ * NE:(q + 1) * NQ * NE],
                                             ecmp.rearrange("p i (a b) -> p (i a) b", b=NE), AX.X, ALU.add)); settle()
                    link(V.tensor_scalar(combf, combf, float(TOPK), None, ALU.is_lt)); settle()
                    link(V.tensor_tensor(combf, combf, sgf, ALU.mult)); settle()
                    link(V.tensor_reduce(wsum, comb, AX.X, ALU.add)); settle()
                    link(V.tensor_scalar(wsum, wsum, 1e-20, None, ALU.add)); settle()
                    link(V.reciprocal(wsum, wsum)); settle()
                    link(V.tensor_tensor(comb, comb, wsum.rearrange("p (i a) -> p i a", a=1)
                                         .broadcast_to([P, NT, NE]), ALU.mult))
                    routed.append(n[0])

                    nh = 0
                    for s in range(NS):
                        c, j = s // NJ, ORDER[s % NJ]
                        dve.wait_ge(sil_done, s + 1)
                        dve.wait_ge(u_mm, s + 1)
                        V.tensor_tensor(hid[:, c, j, :], sil[:, s % 2, :], bank(2 + s % 2), ALU.mult).then_inc(h_made, 1)
                        if j < NE // 2:
                            dve.wait_ge(h_made, s + 1)
                            dve.wait_ge(c_mm, nh + 1)
                            V.tensor_tensor(hid[:, c, j, :], hid[:, c, j, :], bank(4 + nh % 2), ALU.mult)\
                                .then_inc(hc_made, 1)
                            nh += 1
                        if s == NS - 1:
                            for i in range(NT):
                                dve.wait_ge(y_mm, i + 1)
                                V.tensor_copy(ytok[:, i, :], bank(6 + i % 2)[:, 0:C]).then_inc(y_ev, 1)
                    dve.wait_ge(y_ev, NT)
                    close_vector(dve, cs)

                @block.gpsimd
                def _(pool):
                    close_pool(pool, cs)

                @block.scalar
                def _(act):
                    act.wait_ge(lg_mm, 1)
                    nc.scalar.activation(sg.rearrange("p a b -> p (a b)"), bank(6)[:, 0:W], ACT.Exp, scale=-1.0)\
                        .then_inc(lg_exp, 1)
                    for s in range(NS):
                        act.wait_ge(g_mm, s + 1)
                        if s >= 2:
                            act.wait_ge(h_made, s - 1)
                        nc.scalar.activation(sil[:, s % 2, :], bank(s % 2), ACT.Silu).then_inc(sil_done, 1)
                        if s == NE // 4 - 1:
                            act.wait_ge(comb_t, 1)
                            nc.scalar.copy(combT[0:NE, :], bank(4, 2)[0:NE, :]).then_inc(comb_ev, 1)
                    xn_scalar(act, xn_t, xn_ready)

                @block.tensor
                def _(pe):
                    for i in range(NT):
                        for k in range(KC):
                            mm = nc.tensor.matmul(bank(6)[:, i * NE:(i + 1) * NE], xnT[:, k, i * P:(i + 1) * P],
                                                  rwT[:, k, :], start=(k == 0), stop=(k == KC - 1))
                    mm.then_inc(lg_mm, 1)
                    nh = 0
                    for s in range(NS):
                        c, j = s // NJ, ORDER[s % NJ]
                        if s >= 2:
                            pe.wait_ge(sil_done, s - 1)
                        for k in range(KC):
                            mm = nc.tensor.matmul(bank(s % 2), wgT[:, k, j * P:(j + 1) * P],
                                                  xnT[:, k, c * CH:(c + 1) * CH], start=(k == 0), stop=(k == KC - 1))
                        mm.then_inc(g_mm, 1)
                        if s >= 2:
                            pe.wait_ge(h_made, s - 1)
                        for k in range(KC):
                            mm = nc.tensor.matmul(bank(2 + s % 2), wuT[:, k, j * P:(j + 1) * P],
                                                  xnT[:, k, c * CH:(c + 1) * CH], start=(k == 0), stop=(k == KC - 1))
                        mm.then_inc(u_mm, 1)
                        if s == NE // 4 - 1:
                            pe.wait_ge(rt, routed[0])
                            for i in range(NT):
                                mm = nc.tensor.transpose(bank(4, 2)[0:NE, i * P:(i + 1) * P], comb[:, i, :], ident[:])
                            mm.then_inc(comb_t, 1)
                            pe.wait_ge(comb_ev, 1)
                        if j < NE // 2:
                            if nh >= 2:
                                pe.wait_ge(hc_made, nh - 1)
                            nc.tensor.matmul(bank(4 + nh % 2), sel[0:NE, j, :], combT[0:NE, c * CH:(c + 1) * CH],
                                             start=True, stop=True).then_inc(c_mm, 1)
                            nh += 1
                        if s == NS - 1:
                            for i in range(NT):
                                cc = i // (NT // NCH)
                                pe.wait_ge(hc_made, (cc + 1) * NE // 2)
                                pe.wait_ge(h_made, (cc + 1) * NJ)
                                if i >= 2:
                                    pe.wait_ge(y_ev, i - 1)
                                t = i * P - cc * CH
                                for jj in range(NJ):
                                    mm = nc.tensor.matmul(bank(6 + i % 2)[:, 0:C], hid[:, cc, jj, t:t + P],
                                                          wdn[:, jj, :], start=(jj == 0), stop=(jj == NJ - 1))
                                mm.then_inc(y_mm, 1)
                    xn_tensor(pe, applied, NT, xn_t)

            UNITS = [(0, 0), (0, 1), (1, 1), (1, 0)]
            PRE_MM = 2 * NDI + 1 + NDI
            with Phase(nc, "pre_mm pre_ev haloed conv_op conv_done silu_done bc_out bc_b0 bc_b1 bc_c0 bc_c1 sp_e sp_ln sp_t sp_c sp_s sp_sum delta du_done "
                       "dA_done dbu scanned saved cm sig fin gated out_mm out_ev" + CLOSE) as (block, sems):
                (pre_mm, pre_ev, haloed, conv_op, conv_done, silu_done, bc_out, bc_b0, bc_b1, bc_c0, bc_c1, sp_e, sp_ln, sp_t, sp_c, sp_s, sp_sum,
                 delta, du_done, dA_done, dbu, scanned, saved, cm, sig, fin, gated, out_mm, out_ev, *cs) = sems
                stat, aggr, rs_done, applied, added, xn_t, xn_ready = cs

                bc_b, bc_c = (bc_b0, bc_b1), (bc_c0, bc_c1)

                def xi0(d):
                    return TAPS - 1 if d == 0 else 0

                def fwd(d, ap):
                    return ap if d == 0 else ap[:, ::-1]

                @block.sync
                def _(sp):
                    for g in range(len(UNITS)):
                        sp.wait_ge(pre_ev, g * PRE_MM + 2 * NDI + 1)
                        if g >= 2:
                            for c in bc_c:
                                sp.wait_ge(c, 8 * DS * (g - 1))
                        sp.dma_start(bc_scr[g % 2, :, :], xd[DTR:XP, :]).then_inc(bc_out, 16)
                        sp.wait_ge(bc_out, 16 * (g + 1))
                        for n in range(DS):
                            m = g * DS + n
                            if m >= 2:
                                sp.wait_ge(dbu, m - 1)
                            sp.dma_start(Bb[m % 2], bc_scr[g % 2, n:n + 1, :].broadcast_to([P, CH])).then_inc(bc_b[m % 2], 16)
                            if m >= 2:
                                sp.wait_ge(cm, m - 1)
                            sp.dma_start(Cb[m % 2], bc_scr[g % 2, DS + n:DS + n + 1, :].broadcast_to([P, CH]))\
                                .then_inc(bc_c[m % 2], 16)
                    for c in bc_c:
                        sp.wait_ge(c, 8 * DS * len(UNITS))

                @block.tensor
                def _(pe):
                    def pre(g, k):
                        d, c = UNITS[g]
                        b = g % 2
                        xs = slice(c * CH, (c + 1) * CH)
                        if k < 2 * NDI:
                            i = k
                        elif k == 2 * NDI + 1:
                            i = 2 * NDI
                            pe.wait_ge(silu_done, 2 * (g + 1))
                        elif 2 * NDI + 2 <= k < 2 * NDI + 2 + NDI:
                            i = k - 1
                            pe.wait_ge(pre_ev, g * PRE_MM + 2 * NDI + 1)
                        else:
                            return
                        m = g * PRE_MM + i
                        if m >= 2:
                            pe.wait_ge(pre_ev, m - 1)
                        o = bank(4 + m % 2)
                        if i < 2 * NDI:
                            for kk in range(KC):
                                mm = nc.tensor.matmul(o, inT[:, d, kk, i * P:(i + 1) * P], xnT[:, kk, xs],
                                                      start=(kk == 0), stop=(kk == KC - 1))
                        elif i == 2 * NDI:
                            for e in range(NDI):
                                mm = nc.tensor.matmul(o[0:XP, :], xpT[:, d, e, :], u_[b][:, e, :], start=(e == 0),
                                                      stop=(e == NDI - 1))
                        else:
                            e = i - 2 * NDI - 1
                            mm = nc.tensor.matmul(o, dtT[:, d, e * P:(e + 1) * P], xd[0:DTR, :], start=True, stop=True)
                        mm.then_inc(pre_mm, 1)

                    def project(g, tiles):
                        d, c = UNITS[g]
                        pe.wait_ge(gated, g + 1)
                        for t in tiles:
                            m = g * 4 + t
                            if m >= 2:
                                pe.wait_ge(out_ev, m - 1)
                            o = bank(6 + m % 2)[:, 0:C]
                            for e in range(NDI):
                                mm = nc.tensor.matmul(o, sz[g % 2][:, e, t * P:(t + 1) * P], WcT[:, d, e, :],
                                                      start=(e == 0), stop=(d == 1 and e == NDI - 1))
                            if d == 0:
                                for k in range(KC):
                                    tt0 = c * CH + t * P
                                    mm = nc.tensor.matmul(o, xnT[:, k, tt0:tt0 + P], PxT[:, k, :], start=False,
                                                          stop=(k == KC - 1))
                            mm.then_inc(out_mm, 1)

                    for k in range(DS):
                        pre(0, k)
                    for g in range(len(UNITS)):
                        for n in range(DS):
                            if g and n in (2, 3):
                                project(g - 1, (0, 1) if n == 2 else (2, 3))
                            if g + 1 < len(UNITS):
                                pre(g + 1, n)
                            m = g * DS + n
                            pe.wait_ge(cm, m + 1)
                            if n == 0 and g:
                                pe.wait_ge(fin, NDI * g)
                            for e in range(NDI):
                                mm = nc.tensor.matmul(bank(e), ident[:], hb[m % 3][:, e, :], start=(n == 0),
                                                      stop=(n == DS - 1))
                            mm.then_inc(sig, 1)
                    project(len(UNITS) - 1, range(4))
                    xn_tensor(pe, applied, 4 * NT, xn_t)

                @block.scalar
                def _(act):
                    def pre(g, k):
                        d, c = UNITS[g]
                        b = g % 2
                        if k < NDI:
                            if k == 0 and g >= 2:
                                act.wait_ge(dbu, DS * (g - 1))
                            act.wait_ge(pre_mm, g * PRE_MM + k + 1)
                            nc.scalar.copy(du[b][:, k, xi0(d):xi0(d) + CH], bank(4 + (g * PRE_MM + k) % 2))\
                                .then_inc(pre_ev, 1)
                        elif k < 2 * NDI:
                            if k == NDI and g >= 2:
                                act.wait_ge(out_mm, 4 * (g - 1))
                            act.wait_ge(pre_mm, g * PRE_MM + k + 1)
                            nc.scalar.copy(sz[b][:, k - NDI, :], bank(4 + (g * PRE_MM + k) % 2)).then_inc(pre_ev, 1)
                        elif k == 2 * NDI:
                            act.wait_ge(conv_done, NDI * (g + 1))
                            act.wait_ge(pre_ev, g * PRE_MM + 2 * NDI)
                            nc.scalar.activation(u_[b], u_[b], ACT.Silu).then_inc(silu_done, 1)
                            nc.scalar.activation(sz[b], sz[b], ACT.Silu).then_inc(silu_done, 1)
                        elif k == 2 * NDI + 1:
                            act.wait_ge(pre_mm, g * PRE_MM + 2 * NDI + 1)
                            if g:
                                act.wait_ge(bc_out, 16 * g)
                            nc.scalar.copy(xd[0:XP, :], bank(4 + (g * PRE_MM + 2 * NDI) % 2)[0:XP, :])\
                                .then_inc(pre_ev, 1)
                        elif k < 2 * NDI + 2 + NDI:
                            e = k - 2 * NDI - 2
                            m = g * PRE_MM + 2 * NDI + 1 + e
                            q = g * NDI + e
                            bias = dtb[:, d, e:e + 1]
                            act.wait_ge(pre_mm, m + 1)
                            if e == 0:
                                act.wait_ge(haloed, 2 * (g + 1))
                            if g >= 2 and e == 0:
                                act.wait_ge(dA_done, NDI * DS * (g - 1))
                            nc.scalar.activation(du[b][:, e, 0:CH], bank(4 + m % 2), ACT.Abs, bias=bias).then_inc(sp_e, 1)
                            nc.scalar.activation(dl[b][:, e, :], bank(4 + m % 2), ACT.Identity, bias=bias)\
                                .then_inc(pre_ev, 1)
                            act.wait_ge(sp_e, 2 * q + 1)
                            nc.scalar.activation(du[b][:, e, 0:CH], du[b][:, e, 0:CH], ACT.Exp, scale=-1.0)\
                                .then_inc(sp_e, 1)
                            if q >= 2:
                                act.wait_ge(sp_sum, q - 1)
                            act.wait_ge(sp_e, 2 * q + 2)
                            nc.scalar.activation(tl[e % 2], du[b][:, e, 0:CH], ACT.Ln, bias=1.0).then_inc(sp_ln, 1)

                    for k in range(DS):
                        pre(0, k)
                    for g in range(len(UNITS)):
                        d, c = UNITS[g]
                        act.wait_ge(delta, NDI * (g + 1))
                        for n in range(DS):
                            m = g * DS + n
                            if m >= 2:
                                act.wait_ge(scanned, NDI * (m - 1))
                            for e in range(NDI):
                                nc.scalar.activation(dA[m % 2][:, e, :], dl[g % 2][:, e, :], ACT.Exp,
                                                     scale=Aneg[:, d, e, n:n + 1]).then_inc(dA_done, 1)
                            if g + 1 < len(UNITS):
                                pre(g + 1, n)
                    xn_scalar(act, xn_t, xn_ready)

                @block.vector
                def _(dve):
                    V = nc.vector
                    nconv = [0]
                    nhalo = [0]

                    def pre(g, k):
                        d, c = UNITS[g]
                        b = g % 2
                        x0 = xi0(d)
                        h0 = 0 if d == 0 else CH
                        if k == 0:
                            if g >= 2:
                                dve.wait_ge(dbu, DS * (g - 1))
                            dst = du[b][:, :, h0:h0 + TAPS - 1]
                            if g % 2 == 0:
                                V.memset(dst, 0.0).then_inc(haloed, 1)
                            else:
                                V.tensor_copy(dst, halo).then_inc(haloed, 1)
                        if 1 <= k <= NDI:
                            e = k - 1
                            if e == 0:
                                dve.wait_ge(haloed, 2 * g + 1)
                            dve.wait_ge(pre_ev, g * PRE_MM + e + 1)
                            x, o = du[b][:, e, :], u_[b][:, e, :]
                            V.tensor_scalar(o, x[:, x0:x0 + CH], convw[:, d, e, TAPS - 1:TAPS], convb[:, d, e:e + 1],
                                            ALU.mult, ALU.add).then_inc(conv_op, 1)
                            for j in range(1, TAPS):
                                nconv[0] += 1
                                dve.wait_ge(conv_op, nconv[0])
                                s = x0 - j if d == 0 else x0 + j
                                ins = V.scalar_tensor_tensor(out=o, in0=x[:, s:s + CH],
                                                             scalar=convw[:, d, e, TAPS - 1 - j:TAPS - j], in1=o,
                                                             op0=ALU.mult, op1=ALU.add)
                                ins.then_inc(conv_op if j < TAPS - 1 else conv_done, 1)
                            if e == NDI - 1:
                                s = CH + x0 - TAPS + 1 if d == 0 else 0
                                V.tensor_copy(halo, du[b][:, :, s:s + TAPS - 1]).then_inc(haloed, 1)
                        first = 2 * NDI + 3
                        if first <= k < first + NDI:
                            e = k - first
                            q = g * NDI + e
                            dve.wait_ge(sp_ln, q + 1)
                            if q >= 2:
                                dve.wait_ge(sp_c, q - 1)
                                dve.wait_ge(sp_s, q - 1)
                            V.tensor_scalar(tt[e % 2], du[b][:, e, 0:CH], 1.0, -1.0, ALU.add, ALU.add).then_inc(sp_t, 1)
                        if first < k <= first + NDI:
                            softplus_sum(g, k - first - 1)
                        if first + 1 < k:
                            inject(g, k - first - 2)
                        if k == DS - 1:
                            inject(g, NDI - 1)

                    def softplus_sum(g, e):
                        b, q = g % 2, g * NDI + e
                        dve.wait_ge(sp_t, q + 1)
                        V.scalar_tensor_tensor(out=tl[e % 2], in0=tt[e % 2], scalar=0.0, in1=tl[e % 2],
                                               op0=ALU.is_gt, op1=ALU.mult).then_inc(sp_s, 1)
                        dve.wait_ge(sp_s, q + 1)
                        dve.wait_ge(pre_ev, g * PRE_MM + 2 * NDI + 2 + e)
                        V.scalar_tensor_tensor(out=dl[b][:, e, :], in0=dl[b][:, e, :], scalar=0.0, in1=tl[e % 2],
                                               op0=ALU.max, op1=ALU.add).then_inc(sp_sum, 1)

                    def inject(g, e):
                        b, q = g % 2, g * NDI + e
                        dve.wait_ge(delta, q + 1)
                        V.tensor_tensor(du[b][:, e, 0:CH], dl[b][:, e, :], u_[b][:, e, :], ALU.mult).then_inc(du_done, 1)

                    def out_evac(g, tiles):
                        d, c = UNITS[g]
                        for t in tiles:
                            m = g * 4 + t
                            dve.wait_ge(out_mm, m + 1)
                            y = ytok[:, c * 4 + t, :]
                            V.tensor_tensor(y, bank(6 + m % 2)[:, 0:C], pb[:] if d == 0 else y, ALU.add)\
                                .then_inc(out_ev, 1)

                    for k in range(DS):
                        pre(0, k)
                    for g in range(len(UNITS)):
                        d, c = UNITS[g]
                        b = g % 2
                        end = CH - 1 if d == 0 else 0
                        for n in range(DS):
                            m = g * DS + n
                            h = hb[m % 3]
                            dve.wait_ge(dbu, m + 1)
                            for e in range(NDI):
                                dve.wait_ge(dA_done, NDI * m + e + 1)
                                if b == 1:
                                    dve.wait_ge(saved, g // 2 * DS + n + 1)
                                V.tensor_tensor_scan(fwd(d, h[:, e, :]), fwd(d, dA[m % 2][:, e, :]), fwd(d, h[:, e, :]),
                                                     carry[:, n, e:e + 1] if b else 0.0, ALU.mult, ALU.add)\
                                    .then_inc(scanned, 1)
                            dve.wait_ge(scanned, NDI * (m + 1))
                            if b == 0:
                                V.tensor_copy(carry[:, n, :], h[:, :, end]).then_inc(saved, 1)
                                dve.wait_ge(saved, g // 2 * DS + n + 1)
                            dve.wait_ge(bc_c[m % 2], 16 * (m // 2 + 1))
                            V.tensor_tensor(h, h, col(Cb[m % 2]).broadcast_to([P, NDI, CH]), ALU.mult).then_inc(cm, 1)
                            if g and n in (3, 4):
                                out_evac(g - 1, (0, 1) if n == 3 else (2, 3))
                            if g + 1 < len(UNITS):
                                pre(g + 1, n)
                        dve.wait_ge(sig, DS * (g + 1))
                        for e in range(NDI):
                            V.scalar_tensor_tensor(out=u_[b][:, e, :], in0=u_[b][:, e, :], scalar=Dp[:, d, e:e + 1],
                                                   in1=bank(e), op0=ALU.mult, op1=ALU.add).then_inc(fin, 1)
                        dve.wait_ge(fin, NDI * (g + 1))
                        V.tensor_tensor(sz[b], u_[b], sz[b], ALU.mult).then_inc(gated, 1)
                    out_evac(len(UNITS) - 1, range(4))
                    dve.wait_ge(out_ev, 4 * len(UNITS))
                    close_vector(dve, cs, inner=True)

                @block.gpsimd
                def _(pool):
                    def pre(g, k):
                        first = 2 * NDI + 3
                        b = g % 2
                        if first <= k < first + NDI:
                            e = k - first
                            pool.wait_ge(sp_t, g * NDI + e + 1)
                            nc.gpsimd.tensor_tensor(du[b][:, e, 0:CH], du[b][:, e, 0:CH], tt[e % 2], ALU.subtract)\
                                .then_inc(sp_c, 1)
                        if first < k <= first + NDI:
                            e = k - first - 1
                            pool.wait_ge(sp_c, g * NDI + e + 1)
                            pool.wait_ge(sp_sum, g * NDI + e + 1)
                            nc.gpsimd.tensor_tensor(dl[b][:, e, :], dl[b][:, e, :], du[b][:, e, 0:CH], ALU.add)\
                                .then_inc(delta, 1)

                    for k in range(DS):
                        pre(0, k)
                    for g in range(len(UNITS)):
                        pool.wait_ge(du_done, NDI * (g + 1))
                        for n in range(DS):
                            m = g * DS + n
                            pool.wait_ge(bc_b[m % 2], 16 * (m // 2 + 1))
                            if m >= 3:
                                pool.wait_ge(sig, m - 2)
                            nc.gpsimd.tensor_tensor(hb[m % 3], du[g % 2][:, :, 0:CH],
                                                    col(Bb[m % 2]).broadcast_to([P, NDI, CH]), ALU.mult)\
                                .then_inc(dbu, 1)
                            if g + 1 < len(UNITS):
                                pre(g + 1, n)
                    close_pool(pool, cs, inner=True)

            with Phase(nc, "w_in h_mm relu_done sq_done y_mm y_ev x_out" + CLOSE) as (block, sems):
                w_in, h_mm, relu_done, sq_done, y_mm, y_ev, x_out, *cs = sems
                stat, aggr, rs_done, applied, added, xn_t, xn_ready = cs

                @block.sync
                def _(sp):
                    sp.dma_start(wqkT, a["wqkT"]).then_inc(w_in, 16)
                    sp.dma_start(wvT, a["wvT"]).then_inc(w_in, 16)
                    sp.dma_start(woT, a["woT"]).then_inc(w_in, 16)
                    sp.wait_ge(w_in, 48)
                    sp.wait_ge(added, NT)
                    sp.dma_start(out.rearrange("s (i p) c -> (s i) p c", p=P)[bass.ds(seq * NT, NT), :, :]
                                 .rearrange("i p c -> p i c"), xt[:])\
                        .then_inc(x_out, 16)
                    sp.wait_ge(x_out, 16)

                @block.tensor
                def _(pe):
                    def down(c):
                        for t in range(4):
                            i = 4 * c + t
                            pe.wait_ge(sq_done, NF * (c + 1))
                            if i >= 2:
                                pe.wait_ge(y_ev, i - 1)
                            for j in range(NF):
                                mm = nc.tensor.matmul(bank(6 + i % 2)[:, 0:C], r2[c][:, j, t * P:(t + 1) * P],
                                                      WpT[:, j, :], start=(j == 0), stop=(j == NF - 1))
                            mm.then_inc(y_mm, 1)

                    for s in range(NCH * NF):
                        c, j = s // NF, s % NF
                        if s >= 4:
                            pe.wait_ge(sq_done, s - 3)
                        for k in range(KC):
                            mm = nc.tensor.matmul(bank(s % 4), WfT[:, k, j * P:(j + 1) * P],
                                                  xnT[:, k, c * CH:(c + 1) * CH], start=(k == 0), stop=(k == KC - 1))
                        mm.then_inc(h_mm, 1)
                    down(0)
                    down(1)

                @block.scalar
                def _(act):
                    for s in range(NCH * NF):
                        act.wait_ge(h_mm, s + 1)
                        if s >= 2:
                            act.wait_ge(sq_done, s - 1)
                        nc.scalar.activation(rl[:, s % 2, :], bank(s % 4), ACT.Relu).then_inc(relu_done, 1)
                    for i in range(NT):
                        act.wait_ge(y_mm, i + 1)
                        nc.scalar.copy(ytok[:, i, :], bank(6 + i % 2)[:, 0:C]).then_inc(y_ev, 1)

                @block.vector
                def _(dve):
                    for s in range(NCH * NF):
                        dve.wait_ge(relu_done, s + 1)
                        nc.vector.tensor_tensor(r2[s // NF][:, s % NF, :], rl[:, s % 2, :], bank(s % 4), ALU.mult)\
                            .then_inc(sq_done, 1)
                    dve.wait_ge(y_ev, NT)
                    close_vector(dve, cs, last=True)

                @block.gpsimd
                def _(pool):
                    close_pool(pool, cs, last=True)



def kernel(**inputs):
    import concourse.bacc as bacc
    from concourse.bass_utils import run_bass_kernel_spmd as run

    g = {k: np.asarray(v) for k, v in inputs.items()}

    def tiles(w):
        return w.reshape((-1, P) + w.shape[1:]).swapaxes(0, 1)

    def both(name, f):
        return np.stack([f(g[f"L1_attn_{d}_{name}"]) for d in ("fw", "bw")], axis=1)

    row = lambda w: w.reshape(1, -1)
    experts = lambda w: w.transpose(1, 0, 2).reshape(C, NE * HE)
    arrays = {
        "x": g["L0_attn_x"],
        "ident": np.eye(P, dtype=np.float32),
        "tri": np.broadcast_to(np.tril(np.ones((NE, NE), np.float32), -1).reshape(1, -1), (P, NE * NE)),
        "sel": (np.arange(NE)[:, None, None] == 2 * np.arange(NE // 2)[:, None] + np.arange(P) // HE)
        .astype(np.float32),
        "wqkT": tiles(np.concatenate([g["L0_attn_Wq"], g["L0_attn_Wk"]]).T),
        "wvT": tiles(g["L0_attn_Wv"].T), "woT": tiles(g["L0_attn_Wo"].T),
        "brow": row(np.concatenate([g["L0_attn_bq"], g["L0_attn_bk"], g["L0_attn_bv"]])), "bo": row(g["L0_attn_bo"]),
        "rwT": tiles(g["L0_ffn_router_w"].T), "cbias": row(g["L0_ffn_correction_bias"]),
        "wgT": tiles(np.concatenate([experts(g["L0_ffn_gate_w"]), g["L0_ffn_shared_gate_w"].T], axis=1)),
        "wuT": tiles(np.concatenate([experts(g["L0_ffn_up_w"]), g["L0_ffn_shared_up_w"].T], axis=1)),
        "wdn": tiles(np.concatenate([g["L0_ffn_down_w"].reshape(NE * HE, C), g["L0_ffn_shared_down_w"].T])),
        "inT": both("in_w", lambda w: tiles(w.T)),
        "xpT": both("xproj_w", lambda w: tiles(w.T)),
        "dtT": both("dt_w", lambda w: w.T),
        "convw": both("conv_w", lambda w: tiles(w[:, 0, :])),
        "convb": both("conv_b", tiles), "dtb": both("dt_b", tiles), "Dp": both("Dp", tiles),
        "alog": both("Alog", tiles),
        "outw": both("out_w", tiles),
        "projT": np.stack([tiles(g["L1_attn_proj_w"].T[i * C:(i + 1) * C]) for i in range(2)], axis=1),
        "projb": row(g["L1_attn_proj_b"]), "lnw": row(g["L1_attn_ln_w"]), "lnb": row(g["L1_attn_ln_b"]),
        "wfc": tiles(g["L1_ffn_w_fc"]), "wproj": tiles(g["L1_ffn_w_proj"]),
        "uT": g["L1_ffn_u"].T, "v": g["L1_ffn_v"], "fastb": g["L1_ffn_fast_b"],
        "gate": g["L1_ffn_gate"].reshape(1, 1),
    }
    nc = bacc.Bacc("TRN2", target_bir_lowering=False, num_devices=1)
    given, aps = {}, {}
    for name, w in arrays.items():
        w = np.ascontiguousarray(w)
        given[f"in_{name}"] = w
        aps[name] = nc.dram_tensor(f"in_{name}", w.shape, mybir.dt.from_np(w.dtype), kind="ExternalInput").ap()
    out = nc.dram_tensor("out_x", (NSEQ, T, C), F32, kind="ExternalOutput").ap()
    build(nc, aps, out)
    return run(nc, [given], core_ids=[0]).results[0]["out_x"]
```

```python
from contextlib import ExitStack

import concourse.bass as bass
import numpy as np
from concourse import mybir

F32 = mybir.dt.float32
BF16 = mybir.dt.bfloat16
ALU = mybir.AluOpType
ACT = mybir.ActivationFunctionType
AX = mybir.AxisListType

P = 128
NSEQ, T, C = 8, 1024, 256
KC = C // P
NT = T // P
CH = 512
NCH = T // CH
H, D = 16, 16
NE, HE = 16, 64
NG, PG = 4, 4
TOPK, TOPG = 4, 2
HS = 512
NJ = (NE * HE + HS) // P
DI, DS, DTR, TAPS = 512, 16, 16, 4
NDI = DI // P
XP = DTR + 2 * DS
HF, RANK = 1024, 16
NF = HF // P
EPS = 1e-5
ROUND = 12582912.0
BIG = 3.0e38


def col(ap):
    return ap.rearrange("p (a t) -> p a t", a=1)


class Phase:

    def __init__(self, nc, names):
        self.nc, self.names = nc, names.split()

    def __enter__(self):
        self.stack = ExitStack()
        self.sems = [self.stack.enter_context(self.nc.semaphore(n)) for n in self.names]
        self.block = self.stack.enter_context(self.nc.Block())
        return self.block, self.sems

    def __exit__(self, *failed):
        self.stack.close()
        nums = [s.num for s in self.sems]
        if not failed[0]:
            self.nc.all_engine_barrier(sems_to_clear=range(min(nums), max(nums) + 1))


def build(nc, a, out):
    ctx = ExitStack()
    with ctx:
        def sb(name, shape, dt=F32):
            return ctx.enter_context(nc.sbuf_tensor(name, shape, dt))

        xt = sb("xt", [P, NT, C])
        xnT = sb("xnT", [P, KC, T])
        ytok = sb("ytok", [P, NT, C])
        ident = sb("ident", [P, P])
        inT = sb("inT", [P, 2, KC, 2 * DI])
        xpT = sb("xpT", [P, 2, NDI, XP])
        dtT = sb("dtT", [DTR, 2, DI])
        WcT = sb("WcT", [P, 2, NDI, C])
        PxT = sb("PxT", [P, KC, C])
        WfT = sb("WfT", [P, KC, HF])
        WpT = sb("WpT", [P, NF, C])
        bo = sb("bo", [P, C])
        pb = sb("pb", [P, C])
        lnw = sb("lnw", [P, C])
        lnb = sb("lnb", [P, C])
        rwT = sb("rwT", [P, KC, NE])
        cbias = sb("cbias", [P, NE])
        tri = sb("tri", [P, NE, NE])
        ones = sb("ones", [1, P])
        mx = sb("mx", [P, 2, H])
        es = sb("es", [P, 2, H])
        convw = sb("convw", [P, 2, NDI, TAPS])
        convb = sb("convb", [P, 2, NDI])
        dtb = sb("dtb", [P, 2, NDI])
        Dp = sb("Dp", [P, 2, NDI])
        Aneg = sb("Aneg", [P, 2, NDI, DS])
        half = sb("half", [P, NT])
        st = sb("st", [P, NT, 6])
        mv = sb("mv", [P, NT, 2])
        rstd = sb("rstd", [P, NT])
        gatec = sb("gatec", [P, 1])
        KB = 256
        WORK = 126 * KB
        wk = sb("wk", [P, WORK])
        ps = ctx.enter_context(nc.psum_tensor("ps", [P, 8 * CH], F32))

        def area(at, *shape, dt=F32):
            n = int(np.prod(shape)) // (2 if dt == BF16 else 1)
            assert at + n <= WORK, (at, shape)
            v = wk[:, at:at + n]
            v = v if dt == F32 else v.bitcast(dt)
            names = "abcd"[:len(shape)]
            if len(shape) == 1:
                return v
            return v.rearrange("p (%s) -> p %s" % (" ".join(names), " ".join(names)),
                               **{k: s for k, s in zip(names, shape)})

        def bank(i, n=1):
            return ps[:, i * CH:(i + n) * CH]

        prodS = [area((24 + 16 * i) * KB, D, H * H) for i in range(2)]
        prodO = [area((56 + 16 * i) * KB, H, D, H) for i in range(2)]
        qs, ks, vs, Es = [[area((88 + 2 * n + i) * KB, D, H) for i in range(2)] for n in range(4)]
        brow = area(96 * KB, 3 * C)[0:1, :]
        On = [area((124 + i) * KB, C) for i in range(2)]
        An = area(24 * KB, NT, C)
        AnT = area(32 * KB, KC, T)
        wqkT = area(116 * KB, KC, 2 * C)
        wvT = area(120 * KB, KC, C)
        woT = area(122 * KB, KC, C)
        wgT = area(0, KC, NJ * P)
        wuT = area(12 * KB, KC, NJ * P)
        wdn = area(104 * KB, NJ, C)
        sel = area(99 * KB, NE // 2, P)
        hid = area(32 * KB, NCH, NJ, CH)
        sil = area(80 * KB, 2, CH)
        combT = area(84 * KB, T)
        route = area(88 * KB, 11 * KB)
        u_ = [area((8 * i) * KB, NDI, CH) for i in range(2)]
        sz = [area((16 + 8 * i) * KB, NDI, CH) for i in range(2)]
        dl = [area((32 + 8 * i) * KB, NDI, CH) for i in range(2)]
        XW = CH + TAPS
        du = [area(48 * KB + i * NDI * XW, NDI, XW) for i in range(2)]
        at = 48 * KB + 2 * NDI * XW
        hb = [area(at + 8 * KB * i, NDI, CH) for i in range(3)]
        at += 24 * KB
        dA = [area(at + 8 * KB * i, NDI, CH) for i in range(2)]
        at += 16 * KB
        Bb = [area(at + 2 * KB * i, CH) for i in range(2)]
        Cb = [area(at + 4 * KB + 2 * KB * i, CH) for i in range(2)]
        at += 8 * KB
        xd = area(at, CH)
        tl = [area(at + 2 * KB + 2 * KB * i, CH) for i in range(2)]
        tt = [area(at + 6 * KB + 2 * KB * i, CH) for i in range(2)]
        at += 10 * KB
        carry = area(at, DS, NDI)
        halo = area(at + DS * NDI, NDI, TAPS - 1)
        r2 = [area(16 * KB * i, NF, CH) for i in range(2)]
        rl = area(32 * KB, 2, CH)

        o_scr = nc.dram_tensor("o_scr", (H, T, D), F32, kind="Internal").ap()
        bc_scr = nc.dram_tensor("bc_scr", (2, 2 * DS, CH), F32, kind="Internal").ap()

        wl = area(0, NF, C)
        wp = area(8 * KB, KC, HF)
        ow = area(16 * KB, 2, KC, DI)
        pr = area(24 * KB, 2, KC, C)
        uT = area(28 * KB, HF)
        vv = area(32 * KB, C)
        fbt = area(33 * KB, RANK)
        Yr = area(34 * KB, HF)
        sc = area(38 * KB, NF + KC)
        rc = area(38 * KB + 16, NF + KC)
        q_ = area(40 * KB, NF, C)
        qp_ = area(48 * KB, KC, HF)
        alog = area(56 * KB, 2, NDI, DS)
        with Phase(nc, "loaded halved made scaled ternary bit_t bit_c low_mm low_ev comb_mm comb_ev") as (block, sems):
            loaded, halved, made, scaled, ternary, bit_t, bit_c, low_mm, low_ev, comb_mm, comb_ev = sems
            LOADS = [(ident[:], a["ident"]), (tri[:].rearrange("p a b -> p (a b)"), a["tri"]),
                     (inT[:], a["inT"]), (xpT[:], a["xpT"]), (dtT[:], a["dtT"]), (rwT[:], a["rwT"]),
                     (convw[:], a["convw"]), (convb[:], a["convb"]), (dtb[:], a["dtb"]), (Dp[:], a["Dp"]),
                     (wl, a["wfc"]), (wp, a["wproj"]), (ow, a["outw"]), (pr, a["projT"]),
                     (uT[0:RANK, :], a["uT"]), (vv[0:RANK, :], a["v"]), (fbt[0:RANK, :], a["fastb"]),
                     (alog, a["alog"]),
                     (wqkT, a["wqkT"]), (wvT, a["wvT"]), (woT, a["woT"])]
            ROWS = [(bo, "bo"), (pb, "projb"), (lnw, "lnw"), (lnb, "lnb"), (cbias, "cbias"),
                    (gatec, "gate")]
            NLOAD = 16 * (len(LOADS) + len(ROWS))

            @block.sync
            def _(sp):
                for dst, src in LOADS:
                    sp.dma_start(dst, src).then_inc(loaded, 16)
                for dst, name in ROWS:
                    src = a[name]
                    sp.dma_start(dst[:], src.broadcast_to([P, src.shape[1]])).then_inc(loaded, 16)
                sp.wait_ge(loaded, NLOAD)

            @block.gpsimd
            def _(pool):
                nc.gpsimd.memset(half[:], -0.5).then_inc(halved, 1)
                pool.wait_ge(halved, 1)

            @block.scalar
            def _(act):
                act.wait_ge(loaded, NLOAD)
                nc.scalar.activation(Aneg[:], alog, ACT.Exp).then_inc(low_ev, 1)
                act.wait_ge(low_mm, 2)
                nc.scalar.copy(Yr[0:RANK, :], bank(6, 2)[0:RANK, :]).then_inc(low_ev, 1)
                for d in range(2):
                    act.wait_ge(comb_mm, d + 1)
                    nc.scalar.copy(WcT[:, d, :, :].rearrange("p a b -> p (a b)"), bank(4, 2)).then_inc(comb_ev, 1)
                for n in range(2):
                    act.wait_ge(bit_t, n + 1)
                    dst = WfT[:].rearrange("p a b -> p (a b)") if n == 0 else WpT[:].rearrange("p a b -> p (a b)")
                    nc.scalar.copy(dst, bank(0, 4)).then_inc(bit_c, 1)

            @block.vector
            def _(dve):
                dve.wait_ge(loaded, NLOAD)
                nc.vector.memset(ones[:], 1.0).then_inc(made, 1)
                nc.vector.tensor_tensor(PxT[:], pr[:, 0, :, :], pr[:, 1, :, :], ALU.add).then_inc(made, 1)
                dve.wait_ge(low_ev, 1)
                nc.vector.tensor_scalar(Aneg[:], Aneg[:], -1.0, None, ALU.mult).then_inc(made, 1)
                nc.vector.tensor_reduce(sc[:, 0:NF], wl, AX.X, ALU.add, apply_absolute_value=True).then_inc(scaled, 1)
                nc.vector.tensor_reduce(sc[:, NF:], wp, AX.X, ALU.add, apply_absolute_value=True).then_inc(scaled, 1)
                dve.wait_ge(scaled, 2)
                nc.vector.tensor_scalar(sc[:, 0:NF], sc[:, 0:NF], 1.0 / C, 1e-5, ALU.mult, ALU.max).then_inc(scaled, 1)
                nc.vector.tensor_scalar(sc[:, NF:], sc[:, NF:], 1.0 / HF, 1e-5, ALU.mult, ALU.max).then_inc(scaled, 1)
                dve.wait_ge(scaled, 4)
                nc.vector.reciprocal(rc, sc).then_inc(scaled, 1)
                dve.wait_ge(scaled, 5)
                rows = [(wl[:, j, :], q_[:, j, :], j) for j in range(NF)]
                rows += [(wp[:, j, :], qp_[:, j, :], NF + j) for j in range(KC)]
                n = 0
                for w, q, j in rows:
                    nc.vector.tensor_scalar(q, w, rc[:, j:j + 1], ROUND, ALU.mult, ALU.add).then_inc(ternary, 1)
                for w, q, j in rows:
                    dve.wait_ge(ternary, n + len(rows))
                    n += 1
                    nc.vector.tensor_scalar(q, q, -ROUND, 1.0, ALU.add, ALU.min).then_inc(ternary, 1)
                dve.wait_ge(ternary, 2 * len(rows))
                for w, q, j in rows:
                    nc.vector.scalar_tensor_tensor(out=q, in0=q, scalar=-1.0, in1=w, op0=ALU.max,
                                                   op1=ALU.subtract).then_inc(ternary, 1)
                dve.wait_ge(ternary, 3 * len(rows))
                for w, q, j in rows:
                    nc.vector.tensor_tensor(q, q, w, ALU.add).then_inc(ternary, 1)
                dve.wait_ge(ternary, 4 * len(rows))
                for w, q, j in rows:
                    nc.vector.tensor_scalar(q, q, sc[:, j:j + 1], None, ALU.mult).then_inc(ternary, 1)
                for k in range(KC):
                    dve.wait_ge(low_mm, 2 + 2 * (k + 1))
                    dve.wait_ge(bit_c, 1)
                    for c in range(2):
                        w = WfT[:, k, c * CH:(c + 1) * CH]
                        nc.vector.scalar_tensor_tensor(out=w, in0=bank(6 + c), scalar=gatec[:, 0:1], in1=w,
                                                       op0=ALU.mult, op1=ALU.add).then_inc(made, 1)

            @block.tensor
            def _(pe):
                pe.wait_ge(loaded, NLOAD)
                for c in range(2):
                    nc.tensor.matmul(bank(6 + c)[0:RANK, :], fbt[0:RANK, :], uT[0:RANK, c * CH:(c + 1) * CH],
                                     start=True, stop=True).then_inc(low_mm, 1)
                for d in range(2):
                    if d:
                        pe.wait_ge(comb_ev, d)
                    for e in range(NDI):
                        for k in range(KC):
                            mm = nc.tensor.matmul(bank(4, 2)[:, e * C:(e + 1) * C], ow[:, d, k, e * P:(e + 1) * P],
                                                  pr[:, d, k, :], start=(k == 0), stop=(k == KC - 1))
                    mm.then_inc(comb_mm, 1)
                nrow = NF + KC
                pe.wait_ge(ternary, 5 * nrow)
                for k in range(KC):
                    for j in range(NF):
                        mm = nc.tensor.transpose(ps[:, (k * NF + j) * P:(k * NF + j + 1) * P],
                                                 q_[:, j, k * P:(k + 1) * P], ident[:])
                mm.then_inc(bit_t, 1)
                pe.wait_ge(bit_c, 1)
                for j in range(NF):
                    for k in range(KC):
                        mm = nc.tensor.transpose(ps[:, (j * KC + k) * P:(j * KC + k + 1) * P],
                                                 qp_[:, k, j * P:(j + 1) * P], ident[:])
                mm.then_inc(bit_t, 1)
                pe.wait_ge(low_ev, 2)
                for k in range(KC):
                    if k:
                        pe.wait_ge(made, 3 + 2 * k)
                    for c in range(2):
                        nc.tensor.matmul(bank(6 + c), vv[0:RANK, k * P:(k + 1) * P],
                                         Yr[0:RANK, c * CH:(c + 1) * CH], start=True, stop=True).then_inc(low_mm, 1)

        CT = NT // NCH
        CLOSE = " stat aggr rs_done centred applied added xn_t xn_ready"

        def chunk(c):
            return range(c * CT, (c + 1) * CT)

        def ln_stats(dve, s, src, c, nth, made=None):
            stat, aggr = s[0:2]
            for i in chunk(c):
                if made:
                    dve.wait_ge(made, i + 1)
                nc.vector.bn_stats(st[:, i, :], src[:, i, :]).then_inc(stat, 1)
            for i in range(CT):
                dve.wait_ge(stat, nth * CT + i + 1)
                nc.vector.bn_aggr(mv[:, c * CT + i, :], st[:, c * CT + i, :]).then_inc(aggr, 1)

        def ln_rstd(pool, s, c, nth):
            aggr, rs_done = s[1:3]
            rs = rstd[:, c * CT:(c + 1) * CT]
            pool.wait_ge(aggr, (nth + 1) * CT)
            nc.gpsimd.tensor_scalar(rs, mv[:, c * CT:(c + 1) * CT, 1], EPS, None, ALU.add).then_inc(rs_done, 1)
            pool.wait_ge(rs_done, 2 * nth + 1)
            nc.gpsimd.tensor_tensor(rs, rs, half[:, c * CT:(c + 1) * CT], ALU.pow).then_inc(rs_done, 1)

        def ln_apply(dve, s, src, c, nth):
            aggr, rs_done, centred, applied = s[1:5]
            dve.wait_ge(aggr, (nth + 1) * CT)
            dve.wait_ge(rs_done, 2 * (nth + 1))
            for i in chunk(c):
                nc.vector.tensor_scalar(ytok[:, i, :], src[:, i, :], mv[:, i, 0:1], rstd[:, i:i + 1],
                                        ALU.subtract, ALU.mult).then_inc(applied, 1)

        def ln_affine(dve, s, c, nth, naff):
            aggr, rs_done, centred, applied = s[1:5]
            dve.wait_ge(aggr, (nth + 1) * CT)
            for i in chunk(c):
                nc.vector.scalar_tensor_tensor(out=ytok[:, i, :], in0=ytok[:, i, :], scalar=mv[:, i, 0:1],
                                               in1=lnw[:], op0=ALU.subtract, op1=ALU.mult).then_inc(centred, 1)
            dve.wait_ge(rs_done, 2 * (nth + 1))
            for i in range(CT):
                dve.wait_ge(centred, naff * CT + i + 1)
                y = ytok[:, c * CT + i, :]
                nc.vector.scalar_tensor_tensor(out=y, in0=y, scalar=rstd[:, c * CT + i:c * CT + i + 1],
                                               in1=lnb[:], op0=ALU.mult, op1=ALU.add).then_inc(applied, 1)
            dve.wait_ge(applied, (nth + 1) * CT)

        def add_residual(pool, s, c, nth):
            applied, added = s[4:6]
            for i in range(CT):
                pool.wait_ge(applied, nth * CT + i + 1)
                x = xt[:, c * CT + i, :]
                nc.gpsimd.tensor_tensor(x, x, ytok[:, c * CT + i, :], ALU.add).then_inc(added, 1)

        def xn_tensor(pe, s, c, nth, banks):
            applied, added, xn_t = s[4:7]
            for i in range(CT):
                pe.wait_ge(applied, nth * CT + i + 1)
                for k in range(KC):
                    mm = nc.tensor.transpose(bank(banks[k])[:, i * P:(i + 1) * P],
                                             ytok[:, c * CT + i, k * P:(k + 1) * P], ident[:])
            mm.then_inc(xn_t, 1)

        def xn_scalar(act, s, c, nxn, banks):
            xn_t, xn_ready = s[6:8]
            act.wait_ge(xn_t, nxn + 1)
            for k in range(KC):
                nc.scalar.copy(xnT[:, k, c * CH:(c + 1) * CH], bank(banks[k])).then_inc(xn_ready, 1)

        def close_vector(dve, s, n, made, last=False):
            added = s[5]
            ln_stats(dve, s, ytok, 0, n, made)
            ln_apply(dve, s, ytok, 0, n)
            ln_stats(dve, s, ytok, 1, n + 1, made)
            if not last:
                dve.wait_ge(added, CT)
                ln_stats(dve, s, xt, 0, n + 2)
            ln_apply(dve, s, ytok, 1, n + 1)
            if not last:
                ln_apply(dve, s, xt, 0, n + 2)
                dve.wait_ge(added, NT)
                ln_stats(dve, s, xt, 1, n + 3)
                ln_apply(dve, s, xt, 1, n + 3)

        def close_pool(pool, s, n, last=False):
            ln_rstd(pool, s, 0, n)
            add_residual(pool, s, 0, n)
            ln_rstd(pool, s, 1, n + 1)
            if not last:
                ln_rstd(pool, s, 0, n + 2)
            add_residual(pool, s, 1, n + 1)
            if not last:
                ln_rstd(pool, s, 1, n + 3)

        def close_tensor(pe, s, n):
            for c in range(NCH):
                xn_tensor(pe, s, c, n + 2 + c, (c, 2 + c))

        def close_scalar(act, s, first=0):
            for c in range(NCH):
                xn_scalar(act, s, c, first + c, (c, 2 + c))

        with nc.Fori(0, NSEQ) as seq:
            with Phase(nc, "x_in0 x_in1 brow_in moe_in qk_mm v_mm q_ev k_ev v_ev qk_prod s_sum mx_made s_sub exp_done es_made "
                       "rs_made pv_prod pv_sum o_made o_out0 o_out1 an_in an_t ant_ev wo_mm wo_ev" + CLOSE) as (block, sems):
                (x_in0, x_in1, brow_in, moe_in, qk_mm, v_mm, q_ev, k_ev, v_ev, qk_prod, s_sum, mx_made, s_sub, exp_done, es_made,
                 rs_made, pv_prod, pv_sum, o_made, o_out0, o_out1, an_in, an_t, ant_ev, wo_mm, wo_ev, *cs) = sems
                stat, aggr, rs_done, centred, applied, added, xn_t, xn_ready = cs
                o_out, x_in = (o_out0, o_out1), (x_in0, x_in1)

                @block.sync
                def _(sp):
                    for c in range(NCH):
                        sp.dma_start(xt[:, c * CT:(c + 1) * CT, :],
                                     a["x"].rearrange("s (i p) c -> (s i) p c", p=P)[bass.ds(seq * NT + c * CT, CT), :, :]
                                     .rearrange("i p c -> p i c")).then_inc(x_in[c], 16)
                    sp.dma_start(brow, a["brow"]).then_inc(brow_in, 16)
                    sp.dma_start(wgT, a["wgT"]).then_inc(moe_in, 16)
                    sp.dma_start(wuT, a["wuT"]).then_inc(moe_in, 16)
                    sp.dma_start(wdn, a["wdn"]).then_inc(moe_in, 16)
                    sp.dma_start(sel[0:NE, :, :], a["sel"]).then_inc(moe_in, 16)
                    for i in range(NT):
                        sp.wait_ge(o_made, i + 1)
                        sp.dma_start(o_scr[:, i * P:(i + 1) * P, :].rearrange("q t d -> t q d"),
                                     On[i % 2].rearrange("p (q d) -> p q d", d=D)).then_inc(o_out[i % 2], 16)
                    for j in range(2):
                        sp.wait_ge(o_out[j], 16 * (NT // 2))
                    rows = o_scr.rearrange("q (s u) d -> (q s) (u d)", u=C // D)
                    for i in range(NT):
                        if i:
                            sp.wait_ge(an_in, 16 * i)
                        sp.dma_start(An[:, i, :], rows[i * P:(i + 1) * P, :]).then_inc(an_in, 16)
                    sp.wait_ge(an_in, 16 * NT)
                    sp.wait_ge(moe_in, 64)

                @block.tensor
                def _(pe):
                    def project(i):
                        if i >= 2:
                            pe.wait_ge(q_ev, i - 1)
                            pe.wait_ge(k_ev, i - 1)
                            pe.wait_ge(v_ev, i - 1)
                        pe.wait_ge(xn_ready, KC * (i // CT + 1))
                        for k in range(KC):
                            nc.tensor.matmul(bank(4 + i % 2), xnT[:, k, i * P:(i + 1) * P], wqkT[:, k, :],
                                             start=(k == 0), stop=False)
                        nc.tensor.matmul(bank(4 + i % 2), ones[0:1, :], brow[:, 0:2 * C], start=False, stop=True)\
                            .then_inc(qk_mm, 1)
                        for k in range(KC):
                            nc.tensor.matmul(bank(6 + i % 2)[:, 0:C], xnT[:, k, i * P:(i + 1) * P], wvT[:, k, :],
                                             start=(k == 0), stop=False)
                        nc.tensor.matmul(bank(6 + i % 2)[:, 0:C], ones[0:1, :], brow[:, 2 * C:], start=False,
                                         stop=True).then_inc(v_mm, 1)

                    for c in range(NCH):
                        xn_tensor(pe, cs, c, c, (c, 2 + c))
                    pe.wait_ge(brow_in, 16)
                    project(0)
                    project(1)
                    for i in range(NT):
                        pe.wait_ge(qk_prod, i + 1)
                        if i == 0:
                            pe.wait_ge(xn_ready, KC * NCH)
                        if i >= 2:
                            pe.wait_ge(s_sub, i - 1)
                        for d in range(D):
                            mm = nc.tensor.matmul(bank(i % 2)[:, 0:H * H], ident[:], prodS[i % 2][:, d, :],
                                                  start=(d == 0), stop=(d == D - 1))
                        mm.then_inc(s_sum, 1)
                        if i + 2 < NT:
                            project(i + 2)
                    for i in range(NT):
                        pe.wait_ge(an_in, 16 * (i + 1))
                        if i == 0:
                            pe.wait_ge(q_ev, NT)
                            pe.wait_ge(k_ev, NT)
                            pe.wait_ge(s_sub, NT)
                            pe.wait_ge(v_ev, NT)
                        if i >= 2:
                            pe.wait_ge(ant_ev, i - 1)
                        for k in range(KC):
                            mm = nc.tensor.transpose(bank(2 + i % 2)[:, k * P:(k + 1) * P], An[:, i, k * P:(k + 1) * P],
                                                     ident[:])
                        mm.then_inc(an_t, 1)
                    for i in range(NT):
                        pe.wait_ge(ant_ev, i + 1)
                        if i >= 2:
                            pe.wait_ge(wo_ev, i - 1)
                        for k in range(KC):
                            mm = nc.tensor.matmul(bank(6 + i % 2)[:, 0:C], AnT[:, k, i * P:(i + 1) * P], woT[:, k, :],
                                                  start=(k == 0), stop=(k == KC - 1))
                        mm.then_inc(wo_mm, 1)
                    close_tensor(pe, cs, NCH)

                @block.scalar
                def _(act):
                    def by_feature(ap):
                        return ap.rearrange("p (h d) -> p d h", d=D)

                    def spread(i):
                        act.wait_ge(qk_mm, i + 1)
                        if i >= 2:
                            act.wait_ge(qk_prod, i - 1)
                            act.wait_ge(pv_prod, i - 1)
                        nc.scalar.activation(qs[i % 2], by_feature(bank(4 + i % 2)[:, 0:C]), ACT.Copy, scale=0.25)\
                            .then_inc(q_ev, 1)
                        nc.scalar.copy(ks[i % 2], by_feature(bank(4 + i % 2)[:, C:2 * C])).then_inc(k_ev, 1)
                        act.wait_ge(v_mm, i + 1)
                        nc.scalar.copy(vs[i % 2], by_feature(bank(6 + i % 2)[:, 0:C])).then_inc(v_ev, 1)

                    close_scalar(act, cs)
                    spread(0)
                    spread(1)
                    for i in range(NT):
                        act.wait_ge(s_sub, i + 1)
                        e = Es[i % 2].rearrange("p a b -> p (a b)")
                        nc.scalar.activation(e, e, ACT.Exp).then_inc(exp_done, 1)
                        if i + 2 < NT:
                            spread(i + 2)
                    for i in range(NT):
                        act.wait_ge(an_t, i + 1)
                        nc.scalar.copy(AnT[:, :, i * P:(i + 1) * P],
                                       bank(2 + i % 2)[:, 0:C].rearrange("p (k t) -> p k t", k=KC)).then_inc(ant_ev, 1)
                    close_scalar(act, cs, NCH)

                @block.vector
                def _(dve):
                    def products(i):
                        dve.wait_ge(q_ev, i + 1)
                        dve.wait_ge(k_ev, i + 1)
                        if i >= 2:
                            dve.wait_ge(s_sum, i - 1)
                        nc.vector.tensor_tensor(
                            prodS[i % 2].rearrange("p d (q k) -> p d q k", k=H),
                            qs[i % 2].rearrange("p d (q a) -> p d q a", a=1).broadcast_to([P, D, H, H]),
                            ks[i % 2].rearrange("p d (a k) -> p d a k", a=1).broadcast_to([P, D, H, H]),
                            ALU.mult).then_inc(qk_prod, 1)

                    def maxima(i):
                        s = bank(i % 2)[:, 0:H * H].rearrange("p (q k) -> p q k", k=H)
                        dve.wait_ge(s_sum, i + 1)
                        nc.vector.reduce_max(mx[:, i % 2, :], s, AX.X).then_inc(mx_made, 1)
                        dve.wait_ge(mx_made, i + 1)
                        if i >= 2:
                            dve.wait_ge(pv_prod, i - 1)
                            dve.wait_ge(es_made, i - 1)
                        nc.vector.tensor_tensor(Es[i % 2], s, mx[:, i % 2, :].rearrange("p (q a) -> p q a", a=1)
                                                .broadcast_to([P, H, H]), ALU.subtract).then_inc(s_sub, 1)

                    def outputs(i):
                        dve.wait_ge(exp_done, i + 1)
                        nc.vector.reduce_sum(es[:, i % 2, :], Es[i % 2], AX.X).then_inc(es_made, 1)
                        dve.wait_ge(pv_prod, i + 1)
                        if i >= 2:
                            dve.wait_ge(o_out[i % 2], 16 * (i // 2))
                        nc.vector.tensor_reduce(On[i % 2], prodO[i % 2].rearrange("p q d k -> p (q d) k"), AX.X,
                                                ALU.add).then_inc(pv_sum, 1)
                        dve.wait_ge(es_made, i + 1)
                        nc.vector.reciprocal(es[:, i % 2, :], es[:, i % 2, :]).then_inc(rs_made, 1)
                        dve.wait_ge(pv_sum, i + 1)
                        dve.wait_ge(rs_made, i + 1)
                        o = On[i % 2].rearrange("p (q d) -> p q d", d=D)
                        nc.vector.tensor_tensor(o, o, es[:, i % 2, :].rearrange("p (q a) -> p q a", a=1)
                                                .broadcast_to([P, H, D]), ALU.mult).then_inc(o_made, 1)

                    for c in range(NCH):
                        dve.wait_ge(x_in[c], 16)
                        ln_stats(dve, cs, xt, c, c)
                    for c in range(NCH):
                        ln_apply(dve, cs, xt, c, c)
                    products(0)
                    for i in range(NT):
                        if i + 1 < NT:
                            products(i + 1)
                        maxima(i)
                        if i:
                            outputs(i - 1)
                    outputs(NT - 1)
                    for i in range(NT):
                        dve.wait_ge(wo_mm, i + 1)
                        nc.vector.tensor_tensor(ytok[:, i, :], bank(6 + i % 2)[:, 0:C], bo[:], ALU.add)\
                            .then_inc(wo_ev, 1)
                    close_vector(dve, cs, NCH, wo_ev)

                @block.gpsimd
                def _(pool):
                    for c in range(NCH):
                        ln_rstd(pool, cs, c, c)
                    for i in range(NT):
                        pool.wait_ge(exp_done, i + 1)
                        pool.wait_ge(v_ev, i + 1)
                        if i >= 2:
                            pool.wait_ge(pv_sum, i - 1)
                        nc.gpsimd.tensor_tensor(
                            prodO[i % 2],
                            Es[i % 2].rearrange("p q (a k) -> p q a k", a=1).broadcast_to([P, H, D, H]),
                            vs[i % 2].rearrange("p (a d) k -> p a d k", a=1).broadcast_to([P, H, D, H]),
                            ALU.mult).then_inc(pv_prod, 1)
                    close_pool(pool, cs, NCH)

            ORDER = list(range(NE // 2, NJ)) + list(range(NE // 2))
            with Phase(nc, "lg_mm lg_exp rt comb_t comb_ev g_mm u_mm c_mm sil_done h_made hc_made y_mm y_ev"
                       + CLOSE) as (block, sems):
                lg_mm, lg_exp, rt, comb_t, comb_ev, g_mm, u_mm, c_mm, sil_done, h_made, hc_made, y_mm, y_ev, *cs = sems
                stat, aggr, rs_done, centred, applied, added, xn_t, xn_ready = cs
                NS = NCH * NJ
                DOWN = {NJ + 3: (0,), NJ + 5: (1,), NJ + 7: (2,), NJ + 9: (3,), NS - 1: (4, 5, 6, 7)}

                W = NT * NE
                off = [0]
                routed = []

                def rtile(*shape):
                    n = int(np.prod(shape))
                    v = route[:, off[0]:off[0] + n]
                    off[0] += n
                    names = "abcd"[:len(shape)]
                    return v.rearrange("p (%s) -> p %s" % (" ".join(names), " ".join(names)),
                                       **{k: z for k, z in zip(names, shape)}) if len(shape) > 1 else v

                sg = rtile(NT, NE)
                sbv = rtile(NT * NG, PG)
                hi = rtile(NT * NG, 2)
                lo = rtile(NT * NG, 2)
                gs = rtile(NT, NG)
                g2 = rtile(NT * NG)
                gcmp = rtile(NT * NG * NG)
                geq = rtile(NT * NG * NG)
                grank = rtile(NT * NG)
                comb = rtile(NT, NE)
                wsum = rtile(NT)

                NQ = NT // 2
                ecmp = rtile(NQ, NE * NE)
                @block.vector
                def _(dve):
                    n = [0]

                    def link(ins):
                        n[0] += 1
                        ins.then_inc(rt, 1)

                    def settle():
                        dve.wait_ge(rt, n[0])

                    V = nc.vector
                    sgf = sg.rearrange("p a b -> p (a b)")
                    sbf = sbv.rearrange("p a b -> p (a b)")
                    dve.wait_ge(lg_exp, 1)
                    link(V.tensor_scalar(sgf, sgf, 1.0, None, ALU.add)); settle()
                    link(V.reciprocal(sgf, sgf)); settle()
                    link(V.tensor_tensor(sbf.rearrange("p (a b) -> p a b", b=NE), sg,
                                         col(cbias[:]).broadcast_to([P, NT, NE]), ALU.add)); settle()
                    link(V.tensor_tensor(hi, sbv[:, :, 0:2], sbv[:, :, 2:4], ALU.max))
                    link(V.tensor_tensor(lo, sbv[:, :, 0:2], sbv[:, :, 2:4], ALU.min)); settle()
                    link(V.tensor_tensor(g2, hi[:, :, 0], hi[:, :, 1], ALU.min))
                    link(V.tensor_tensor(hi[:, :, 0], hi[:, :, 0], hi[:, :, 1], ALU.max))
                    link(V.tensor_tensor(lo[:, :, 0], lo[:, :, 0], lo[:, :, 1], ALU.max)); settle()
                    link(V.tensor_tensor(g2, g2, lo[:, :, 0], ALU.max)); settle()
                    link(V.tensor_tensor(gs.rearrange("p a b -> p (a b)"), hi[:, :, 0], g2, ALU.add)); settle()
                    for i in range(NT):
                        o = gcmp[:, i * NG * NG:(i + 1) * NG * NG].rearrange("p (a b) -> p a b", a=NG)
                        e = geq[:, i * NG * NG:(i + 1) * NG * NG].rearrange("p (a b) -> p a b", a=NG)
                        other = col(gs[:, i, :]).broadcast_to([P, NG, NG])
                        own = gs[:, i, :].rearrange("p (a b) -> p a b", b=1).broadcast_to([P, NG, NG])
                        link(V.tensor_tensor(o, other, own, ALU.is_gt))
                        link(V.tensor_tensor(e, other, own, ALU.is_equal))
                    settle()
                    e4 = geq.rearrange("p (i a b) -> p i a b", a=NG, b=NG)
                    for i in range(NT):
                        link(V.tensor_tensor(e4[:, i, :, :], e4[:, i, :, :], tri[:, 0:NG, 0:NG], ALU.mult))
                    settle()
                    link(V.tensor_tensor(gcmp, gcmp, geq, ALU.add)); settle()
                    link(V.tensor_reduce(grank, gcmp.rearrange("p (g b) -> p g b", b=NG), AX.X, ALU.add)); settle()
                    link(V.tensor_scalar(grank, grank, float(TOPG), None, ALU.is_lt)); settle()
                    mask = grank.rearrange("p (g a) -> p g a", a=1).broadcast_to([P, NT * NG, PG])
                    link(V.tensor_tensor(sbv, sbv, mask, ALU.mult))
                    link(V.tensor_scalar(g2, grank, BIG, -BIG, ALU.mult, ALU.add)); settle()
                    link(V.tensor_tensor(sbv, sbv, g2.rearrange("p (g a) -> p g a", a=1)
                                         .broadcast_to([P, NT * NG, PG]), ALU.add)); settle()
                    eq_ = hid[:, 1, 0:2, :].rearrange("p a b -> p (a b)")
                    combf = comb.rearrange("p a b -> p (a b)")
                    for q in range(NT // NQ):
                        for i in range(NQ):
                            m = sbf[:, (q * NQ + i) * NE:(q * NQ + i + 1) * NE]
                            other = col(m).broadcast_to([P, NE, NE])
                            own = m.rearrange("p (a b) -> p a b", b=1).broadcast_to([P, NE, NE])
                            link(V.tensor_tensor(ecmp[:, i, :].rearrange("p (a b) -> p a b", a=NE), other, own, ALU.is_gt))
                            link(V.tensor_tensor(eq_[:, i * NE * NE:(i + 1) * NE * NE]
                                                 .rearrange("p (a b) -> p a b", a=NE), other, own, ALU.is_equal))
                        settle()
                        eqs = eq_[:, 0:NQ * NE * NE].rearrange("p (i a) -> p i a", i=NQ)
                        link(V.tensor_tensor(eqs, eqs, col(tri[:].rearrange("p a b -> p (a b)"))
                                             .broadcast_to([P, NQ, NE * NE]), ALU.mult)); settle()
                        link(V.tensor_tensor(ecmp, ecmp, eqs, ALU.add)); settle()
                        link(V.tensor_reduce(combf[:, q * NQ * NE:(q + 1) * NQ * NE],
                                             ecmp.rearrange("p i (a b) -> p (i a) b", b=NE), AX.X, ALU.add)); settle()
                    link(V.tensor_scalar(combf, combf, float(TOPK), None, ALU.is_lt)); settle()
                    link(V.tensor_tensor(combf, combf, sgf, ALU.mult)); settle()
                    link(V.tensor_reduce(wsum, comb, AX.X, ALU.add)); settle()
                    link(V.tensor_scalar(wsum, wsum, 1e-20, None, ALU.add)); settle()
                    link(V.reciprocal(wsum, wsum)); settle()
                    link(V.tensor_tensor(comb, comb, wsum.rearrange("p (i a) -> p i a", a=1)
                                         .broadcast_to([P, NT, NE]), ALU.mult))
                    routed.append(n[0])

                    nh = 0
                    for s in range(NS):
                        c, j = s // NJ, ORDER[s % NJ]
                        dve.wait_ge(sil_done, s + 1)
                        dve.wait_ge(u_mm, s + 1)
                        V.tensor_tensor(hid[:, c, j, :], sil[:, s % 2, :], bank(2 + s % 2), ALU.mult).then_inc(h_made, 1)
                        if j < NE // 2:
                            dve.wait_ge(h_made, s + 1)
                            dve.wait_ge(c_mm, nh + 1)
                            V.tensor_tensor(hid[:, c, j, :], hid[:, c, j, :], bank(4 + nh % 2), ALU.mult)\
                                .then_inc(hc_made, 1)
                            nh += 1
                    close_vector(dve, cs, 0, y_ev)

                @block.gpsimd
                def _(pool):
                    close_pool(pool, cs, 0)

                @block.scalar
                def _(act):
                    act.wait_ge(lg_mm, 1)
                    nc.scalar.activation(sg.rearrange("p a b -> p (a b)"), bank(6)[:, 0:W], ACT.Exp, scale=-1.0)\
                        .then_inc(lg_exp, 1)
                    for s in range(NS):
                        act.wait_ge(g_mm, s + 1)
                        if s >= 2:
                            act.wait_ge(h_made, s - 1)
                        nc.scalar.activation(sil[:, s % 2, :], bank(s % 2), ACT.Silu).then_inc(sil_done, 1)
                        if s == NE // 4 - 1:
                            act.wait_ge(comb_t, 1)
                            nc.scalar.copy(combT[0:NE, :], bank(4, 2)[0:NE, :]).then_inc(comb_ev, 1)
                        for i in DOWN.get(s, ()):
                            act.wait_ge(y_mm, i + 1)
                            nc.scalar.copy(ytok[:, i, :], bank(6 + i % 2)[:, 0:C]).then_inc(y_ev, 1)
                    close_scalar(act, cs)

                @block.tensor
                def _(pe):
                    for i in range(NT):
                        for k in range(KC):
                            mm = nc.tensor.matmul(bank(6)[:, i * NE:(i + 1) * NE], xnT[:, k, i * P:(i + 1) * P],
                                                  rwT[:, k, :], start=(k == 0), stop=(k == KC - 1))
                    mm.then_inc(lg_mm, 1)
                    nh = 0
                    for s in range(NS):
                        c, j = s // NJ, ORDER[s % NJ]
                        if s >= 2:
                            pe.wait_ge(sil_done, s - 1)
                        for k in range(KC):
                            mm = nc.tensor.matmul(bank(s % 2), wgT[:, k, j * P:(j + 1) * P],
                                                  xnT[:, k, c * CH:(c + 1) * CH], start=(k == 0), stop=(k == KC - 1))
                        mm.then_inc(g_mm, 1)
                        if s >= 2:
                            pe.wait_ge(h_made, s - 1)
                        for k in range(KC):
                            mm = nc.tensor.matmul(bank(2 + s % 2), wuT[:, k, j * P:(j + 1) * P],
                                                  xnT[:, k, c * CH:(c + 1) * CH], start=(k == 0), stop=(k == KC - 1))
                        mm.then_inc(u_mm, 1)
                        if s == NE // 4 - 1:
                            pe.wait_ge(rt, routed[0])
                            for i in range(NT):
                                mm = nc.tensor.transpose(bank(4, 2)[0:NE, i * P:(i + 1) * P], comb[:, i, :], ident[:])
                            mm.then_inc(comb_t, 1)
                            pe.wait_ge(comb_ev, 1)
                        if j < NE // 2:
                            if nh >= 2:
                                pe.wait_ge(hc_made, nh - 1)
                            nc.tensor.matmul(bank(4 + nh % 2), sel[0:NE, j, :], combT[0:NE, c * CH:(c + 1) * CH],
                                             start=True, stop=True).then_inc(c_mm, 1)
                            nh += 1
                        for i in DOWN.get(s, ()):
                            pe.wait_ge(hc_made, (i // CT + 1) * NE // 2)
                            pe.wait_ge(h_made, (i // CT + 1) * NJ)
                            if i >= 2:
                                pe.wait_ge(y_ev, i - 1)
                            t = i % CT * P
                            for jj in range(NJ):
                                mm = nc.tensor.matmul(bank(6 + i % 2)[:, 0:C], hid[:, i // CT, jj, t:t + P],
                                                      wdn[:, jj, :], start=(jj == 0), stop=(jj == NJ - 1))
                            mm.then_inc(y_mm, 1)
                    close_tensor(pe, cs, 0)

            UNITS = [(0, 0), (0, 1), (1, 1), (1, 0)]
            NU = len(UNITS)
            X0, Z0, XD, L0 = 0, NDI, 2 * NDI, 2 * NDI + 1
            NPRE = L0 + NDI
            PRE_PE = {0: (0, 1), 1: (2,), 2: (3,), 3: (4,), 4: (5,), 5: (6,), 6: (7,), 8: (8,), 10: (9, 10, 11), 11: (12,)}
            PRE_ACT = {2: (0, 1), 3: (2,), 4: (3,), 5: (4,), 6: (5,), 7: (6,), 8: (7,), 10: (8,), 12: (9, 10), 13: (11, 12)}
            CONV = {2: 0, 3: 1, 4: 2, 5: 3}
            SILU_U, SILU_Z = 7, 8
            TERM = {12: (0, 1), 13: (2, 3)}
            SUM = {13: (0, 1), 14: (2, 3)}
            LOST = {14: (0, 1), 15: (2, 3)}
            DELTA = {15: (0, 1)}
            OUT = {2: 0, 3: 1, 4: 2, 5: 3}
            CLOSE_DVE = {6: "stats0", 8: "apply0", 9: "stats1", 11: "apply1", 13: "stats2", 15: "apply2"}
            CLOSE_POOL = {8: "rstd0", 11: "rstd1", 13: "add", 15: "rstd2"}
            with Phase(nc, "pre_mm pre_ev haloed conv_op conv_done silu_u silu_z bc_out bc_b0 bc_b1 bc_c0 bc_c1 sp_e sp_ln "
                       "sp_t sp_c sp_s sp_sum delta du_done dA_done dbu scanned saved cm sig fin gated out_mm out_ev"
                       + CLOSE) as (block, sems):
                (pre_mm, pre_ev, haloed, conv_op, conv_done, silu_u, silu_z, bc_out, bc_b0, bc_b1, bc_c0, bc_c1, sp_e, sp_ln,
                 sp_t, sp_c, sp_s, sp_sum, delta, du_done, dA_done, dbu, scanned, saved, cm, sig, fin, gated, out_mm,
                 out_ev, *cs) = sems
                stat, aggr, rs_done, centred, applied, added, xn_t, xn_ready = cs

                bc_b, bc_c = (bc_b0, bc_b1), (bc_c0, bc_c1)

                def xi0(d):
                    return TAPS - 1 if d == 0 else 0

                def fwd(d, ap):
                    return ap if d == 0 else ap[:, ::-1]

                def pre_bank(m):
                    return bank(4 + m % 3)

                def out_bank(g, t):
                    return bank(7 if g < NU - 1 else 4 + t)[:, 0:C]

                @block.sync
                def _(sp):
                    for g in range(NU):
                        sp.wait_ge(pre_ev, g * NPRE + XD + 1)
                        if g >= 2:
                            for c in bc_c:
                                sp.wait_ge(c, 8 * DS * (g - 1))
                        sp.dma_start(bc_scr[g % 2, :, :], xd[DTR:XP, :]).then_inc(bc_out, 16)
                        sp.wait_ge(bc_out, 16 * (g + 1))
                        for n in range(DS):
                            m = g * DS + n
                            if m >= 2:
                                sp.wait_ge(dbu, m - 1)
                            sp.dma_start(Bb[m % 2], bc_scr[g % 2, n:n + 1, :].broadcast_to([P, CH])).then_inc(bc_b[m % 2], 16)
                            if m >= 2:
                                sp.wait_ge(cm, m - 1)
                            sp.dma_start(Cb[m % 2], bc_scr[g % 2, DS + n:DS + n + 1, :].broadcast_to([P, CH]))\
                                .then_inc(bc_c[m % 2], 16)
                    for c in bc_c:
                        sp.wait_ge(c, 8 * DS * NU)

                @block.tensor
                def _(pe):
                    def pre(g, i):
                        d, c = UNITS[g]
                        b = g % 2
                        xs = slice(c * CH, (c + 1) * CH)
                        m = g * NPRE + i
                        if i == XD:
                            pe.wait_ge(silu_u, g + 1)
                        if i == L0:
                            pe.wait_ge(pre_ev, g * NPRE + XD + 1)
                        if m >= 3:
                            pe.wait_ge(pre_ev, m - 2)
                        o = pre_bank(m)
                        if i < XD:
                            for k in range(KC):
                                mm = nc.tensor.matmul(o, inT[:, d, k, i * P:(i + 1) * P], xnT[:, k, xs],
                                                      start=(k == 0), stop=(k == KC - 1))
                        elif i == XD:
                            for e in range(NDI):
                                mm = nc.tensor.matmul(o[0:XP, :], xpT[:, d, e, :], u_[b][:, e, :], start=(e == 0),
                                                      stop=(e == NDI - 1))
                        else:
                            e = i - L0
                            mm = nc.tensor.matmul(o, dtT[:, d, e * P:(e + 1) * P], xd[0:DTR, :], start=True, stop=True)
                        mm.then_inc(pre_mm, 1)

                    def project(g, t):
                        d, c = UNITS[g]
                        if t == 0:
                            pe.wait_ge(gated, g + 1)
                        if g < NU - 1 and g * CT + t:
                            pe.wait_ge(out_ev, g * CT + t)
                        o = out_bank(g, t)
                        for e in range(NDI):
                            mm = nc.tensor.matmul(o, sz[g % 2][:, e, t * P:(t + 1) * P], WcT[:, d, e, :],
                                                  start=(e == 0), stop=(d == 1 and e == NDI - 1))
                        if d == 0:
                            t0 = c * CH + t * P
                            for k in range(KC):
                                mm = nc.tensor.matmul(o, xnT[:, k, t0:t0 + P], PxT[:, k, :], start=False,
                                                      stop=(k == KC - 1))
                        mm.then_inc(out_mm, 1)

                    for n in range(DS):
                        for i in PRE_PE.get(n, ()):
                            pre(0, i)
                    for g in range(NU):
                        for n in range(DS):
                            if g + 1 < NU:
                                for i in PRE_PE.get(n, ()):
                                    pre(g + 1, i)
                            if g and n in OUT:
                                project(g - 1, OUT[n])
                            m = g * DS + n
                            pe.wait_ge(cm, m + 1)
                            if n == 0 and g:
                                pe.wait_ge(fin, NDI * g)
                            for e in range(NDI):
                                mm = nc.tensor.matmul(bank(e), ident[:], hb[m % 3][:, e, :], start=(n == 0),
                                                      stop=(n == DS - 1))
                            mm.then_inc(sig, 1)
                    xn_tensor(pe, cs, 1, 2, (4, 5))
                    pe.wait_ge(xn_ready, KC)
                    pe.wait_ge(out_ev, (NU - 1) * CT)
                    for t in range(CT):
                        project(NU - 1, t)
                    pe.wait_ge(fin, NDI * NU)
                    xn_tensor(pe, cs, 0, 5, (0, 1))

                @block.scalar
                def _(act):
                    def pre(g, items):
                        d, c = UNITS[g]
                        b = g % 2
                        for i in items:
                            m = g * NPRE + i
                            act.wait_ge(pre_mm, m + 1)
                            if i < Z0:
                                if i == X0 and g >= 2:
                                    act.wait_ge(dbu, DS * (g - 1))
                                nc.scalar.copy(du[b][:, i, xi0(d):xi0(d) + CH], pre_bank(m)).then_inc(pre_ev, 1)
                            elif i < XD:
                                if i == Z0 and g >= 2:
                                    act.wait_ge(out_mm, CT * (g - 1))
                                nc.scalar.copy(sz[b][:, i - Z0, :], pre_bank(m)).then_inc(pre_ev, 1)
                            elif i == XD:
                                if g:
                                    act.wait_ge(bc_out, 16 * g)
                                nc.scalar.copy(xd[0:XP, :], pre_bank(m)[0:XP, :]).then_inc(pre_ev, 1)
                            else:
                                e = i - L0
                                bias = dtb[:, d, e:e + 1]
                                if e == 0:
                                    act.wait_ge(haloed, 2 * (g + 1))
                                    if g >= 2:
                                        act.wait_ge(dA_done, NDI * DS * (g - 1))
                                nc.scalar.activation(du[b][:, e, 0:CH], pre_bank(m), ACT.Abs, bias=bias).then_inc(sp_e, 1)
                                nc.scalar.activation(dl[b][:, e, :], pre_bank(m), ACT.Identity, bias=bias)\
                                    .then_inc(pre_ev, 1)
                        if items and items[0] >= L0:
                            q = g * NDI + items[0] - L0
                            for j in range(2):
                                e = items[j] - L0
                                act.wait_ge(sp_e, 2 * q + 1 + j)
                                nc.scalar.activation(du[b][:, e, 0:CH], du[b][:, e, 0:CH], ACT.Exp, scale=-1.0)\
                                    .then_inc(sp_e, 1)
                            for j in range(2):
                                e = items[j] - L0
                                if q:
                                    act.wait_ge(sp_sum, q - 1 + j)
                                act.wait_ge(sp_e, 2 * q + 3 + j)
                                nc.scalar.activation(tl[e % 2], du[b][:, e, 0:CH], ACT.Ln, bias=1.0).then_inc(sp_ln, 1)

                    def silus(g, n):
                        if n == SILU_U:
                            act.wait_ge(conv_done, NDI * (g + 1))
                            nc.scalar.activation(u_[g % 2], u_[g % 2], ACT.Silu).then_inc(silu_u, 1)
                        if n == SILU_Z:
                            act.wait_ge(pre_ev, g * NPRE + XD)
                            nc.scalar.activation(sz[g % 2], sz[g % 2], ACT.Silu).then_inc(silu_z, 1)

                    for n in range(DS):
                        pre(0, PRE_ACT.get(n, ()))
                        silus(0, n)
                    for g in range(NU):
                        d, c = UNITS[g]
                        act.wait_ge(delta, NDI * (g + 1))
                        for n in range(DS):
                            m = g * DS + n
                            if m >= 2:
                                act.wait_ge(scanned, NDI * (m - 1))
                            for e in range(NDI):
                                nc.scalar.activation(dA[m % 2][:, e, :], dl[g % 2][:, e, :], ACT.Exp,
                                                     scale=Aneg[:, d, e, n:n + 1]).then_inc(dA_done, 1)
                            if g + 1 < NU:
                                pre(g + 1, PRE_ACT.get(n, ()))
                                silus(g + 1, n)
                    xn_scalar(act, cs, 1, 0, (4, 5))
                    xn_scalar(act, cs, 0, 1, (0, 1))

                @block.vector
                def _(dve):
                    V = nc.vector
                    nconv = [0]

                    def conv(g, e):
                        d, c = UNITS[g]
                        b, x0 = g % 2, xi0(d)
                        if e == 0:
                            dve.wait_ge(haloed, 2 * g + 1)
                            if g >= 2:
                                dve.wait_ge(fin, NDI * (g - 1))
                        dve.wait_ge(pre_ev, g * NPRE + X0 + e + 1)
                        x, o = du[b][:, e, :], u_[b][:, e, :]
                        V.tensor_scalar(o, x[:, x0:x0 + CH], convw[:, d, e, TAPS - 1:TAPS], convb[:, d, e:e + 1],
                                        ALU.mult, ALU.add).then_inc(conv_op, 1)
                        for j in range(1, TAPS):
                            nconv[0] += 1
                            dve.wait_ge(conv_op, nconv[0])
                            s = x0 - j if d == 0 else x0 + j
                            ins = V.scalar_tensor_tensor(out=o, in0=x[:, s:s + CH],
                                                         scalar=convw[:, d, e, TAPS - 1 - j:TAPS - j], in1=o,
                                                         op0=ALU.mult, op1=ALU.add)
                            ins.then_inc(conv_op if j < TAPS - 1 else conv_done, 1)
                        if e == NDI - 1:
                            s = CH + x0 - TAPS + 1 if d == 0 else 0
                            V.tensor_copy(halo, du[b][:, :, s:s + TAPS - 1]).then_inc(haloed, 1)

                    def pre(g, n):
                        d, c = UNITS[g]
                        b = g % 2
                        if n == 1:
                            h0 = 0 if d == 0 else CH
                            if g >= 2:
                                dve.wait_ge(dbu, DS * (g - 1))
                            dst = du[b][:, :, h0:h0 + TAPS - 1]
                            if g % 2 == 0:
                                V.memset(dst, 0.0).then_inc(haloed, 1)
                            else:
                                dve.wait_ge(haloed, 2 * g)
                                V.tensor_copy(dst, halo).then_inc(haloed, 1)
                        if n in CONV:
                            conv(g, CONV[n])
                        for e in SUM.get(n, ()):
                            q = g * NDI + e
                            dve.wait_ge(sp_t, q + 1)
                            V.scalar_tensor_tensor(out=tl[e % 2], in0=tt[e % 2], scalar=0.0, in1=tl[e % 2],
                                                   op0=ALU.is_gt, op1=ALU.mult).then_inc(sp_s, 1)
                        for e in SUM.get(n, ()):
                            q = g * NDI + e
                            dve.wait_ge(sp_s, q + 1)
                            dve.wait_ge(pre_ev, g * NPRE + L0 + e + 1)
                            V.scalar_tensor_tensor(out=dl[b][:, e, :], in0=dl[b][:, e, :], scalar=0.0, in1=tl[e % 2],
                                                   op0=ALU.max, op1=ALU.add).then_inc(sp_sum, 1)
                        for e in TERM.get(n, ()):
                            q = g * NDI + e
                            dve.wait_ge(sp_ln, q + 1)
                            if q >= 2:
                                dve.wait_ge(sp_c, q - 1)
                                dve.wait_ge(sp_s, q - 1)
                            V.tensor_scalar(tt[e % 2], du[b][:, e, 0:CH], 1.0, -1.0, ALU.add, ALU.add).then_inc(sp_t, 1)
                        if n == DS - 1:
                            for e in range(NDI):
                                dve.wait_ge(delta, g * NDI + e + 1)
                                V.tensor_tensor(du[b][:, e, 0:CH], dl[b][:, e, :], u_[b][:, e, :], ALU.mult)\
                                    .then_inc(du_done, 1)

                    def out_evac(g, t):
                        d, c = UNITS[g]
                        dve.wait_ge(out_mm, g * CT + t + 1)
                        y = ytok[:, c * CT + t, :]
                        V.tensor_tensor(y, out_bank(g, t), pb[:] if d == 0 else y, ALU.add).then_inc(out_ev, 1)

                    def close_step(c, name, nth, naff):
                        what, level = name[:-1], int(name[-1])
                        if what == "stats":
                            if level == 2:
                                dve.wait_ge(added, CT * (naff + 1))
                            ln_stats(dve, cs, xt if level == 2 else ytok, c, nth + level)
                        elif level == 0:
                            ln_affine(dve, cs, c, nth, naff)
                        else:
                            ln_apply(dve, cs, xt if level == 2 else ytok, c, nth + level)

                    for n in range(DS):
                        pre(0, n)
                    for g in range(NU):
                        d, c = UNITS[g]
                        b = g % 2
                        end = CH - 1 if d == 0 else 0
                        for n in range(DS):
                            m = g * DS + n
                            h = hb[m % 3]
                            dve.wait_ge(dbu, m + 1)
                            for e in range(NDI):
                                dve.wait_ge(dA_done, NDI * m + e + 1)
                                if b == 1:
                                    dve.wait_ge(saved, g // 2 * DS + n + 1)
                                V.tensor_tensor_scan(fwd(d, h[:, e, :]), fwd(d, dA[m % 2][:, e, :]), fwd(d, h[:, e, :]),
                                                     carry[:, n, e:e + 1] if b else 0.0, ALU.mult, ALU.add)\
                                    .then_inc(scanned, 1)
                            dve.wait_ge(scanned, NDI * (m + 1))
                            if b == 0:
                                V.tensor_copy(carry[:, n, :], h[:, :, end]).then_inc(saved, 1)
                                dve.wait_ge(saved, g // 2 * DS + n + 1)
                            dve.wait_ge(bc_c[m % 2], 16 * (m // 2 + 1))
                            V.tensor_tensor(h, h, col(Cb[m % 2]).broadcast_to([P, NDI, CH]), ALU.mult).then_inc(cm, 1)
                            if g + 1 < NU:
                                pre(g + 1, n)
                            if g and n in OUT:
                                out_evac(g - 1, OUT[n])
                                if g == NU - 1 and OUT[n] == CT - 1:
                                    dve.wait_ge(out_ev, (NU - 1) * CT)
                            if g == NU - 1 and n in CLOSE_DVE:
                                close_step(1, CLOSE_DVE[n], 0, 0)
                        dve.wait_ge(sig, DS * (g + 1))
                        for e in range(NDI):
                            V.scalar_tensor_tensor(out=u_[b][:, e, :], in0=u_[b][:, e, :], scalar=Dp[:, d, e:e + 1],
                                                   in1=bank(e), op0=ALU.mult, op1=ALU.add).then_inc(fin, 1)
                        dve.wait_ge(silu_z, g + 1)
                        dve.wait_ge(fin, NDI * (g + 1))
                        V.tensor_tensor(sz[b], u_[b], sz[b], ALU.mult).then_inc(gated, 1)
                    for t in range(CT):
                        out_evac(NU - 1, t)
                    dve.wait_ge(out_ev, CT * NU)
                    for name in ("stats0", "apply0", "stats1", "apply1", "stats2", "apply2"):
                        close_step(0, name, 3, 1)

                @block.gpsimd
                def _(pool):
                    def pre(g, n):
                        b = g % 2
                        for e in DELTA.get(n, ()) if n < DS else (2, 3):
                            pool.wait_ge(sp_c, g * NDI + e + 1)
                            pool.wait_ge(sp_sum, g * NDI + e + 1)
                            nc.gpsimd.tensor_tensor(dl[b][:, e, :], dl[b][:, e, :], du[b][:, e, 0:CH], ALU.add)\
                                .then_inc(delta, 1)
                        for e in LOST.get(n, ()):
                            pool.wait_ge(sp_t, g * NDI + e + 1)
                            nc.gpsimd.tensor_tensor(du[b][:, e, 0:CH], du[b][:, e, 0:CH], tt[e % 2], ALU.subtract)\
                                .then_inc(sp_c, 1)

                    def close_step(c, name, nth, nadd):
                        if name == "add":
                            add_residual(pool, cs, c, nth + 1)
                        else:
                            ln_rstd(pool, cs, c, nth + int(name[-1]))

                    for n in range(DS + 1):
                        pre(0, n)
                    for g in range(NU):
                        pool.wait_ge(du_done, NDI * (g + 1))
                        for n in range(DS):
                            m = g * DS + n
                            pool.wait_ge(bc_b[m % 2], 16 * (m // 2 + 1))
                            if m >= 3:
                                pool.wait_ge(sig, m - 2)
                            nc.gpsimd.tensor_tensor(hb[m % 3], du[g % 2][:, :, 0:CH],
                                                    col(Bb[m % 2]).broadcast_to([P, NDI, CH]), ALU.mult)\
                                .then_inc(dbu, 1)
                            if g + 1 < NU:
                                pre(g + 1, n)
                            elif n in CLOSE_POOL:
                                close_step(1, CLOSE_POOL[n], 0, 0)
                        if g + 1 < NU:
                            pre(g + 1, DS)
                    for name in ("rstd0", "rstd1", "add", "rstd2"):
                        close_step(0, name, 3, 1)

            with Phase(nc, "w_in h_mm relu_done sq_done y_mm y_ev x_out" + CLOSE) as (block, sems):
                w_in, h_mm, relu_done, sq_done, y_mm, y_ev, x_out, *cs = sems
                stat, aggr, rs_done, centred, applied, added, xn_t, xn_ready = cs
                DOWN = {NF + 1: (0,), NF + 3: (1,), NF + 5: (2,), NF + 7: (3, 4, 5, 6, 7)}

                @block.sync
                def _(sp):
                    sp.dma_start(wqkT, a["wqkT"]).then_inc(w_in, 16)
                    sp.dma_start(wvT, a["wvT"]).then_inc(w_in, 16)
                    sp.dma_start(woT, a["woT"]).then_inc(w_in, 16)
                    for c in range(NCH):
                        sp.wait_ge(added, CT * (c + 1))
                        sp.dma_start(out.rearrange("s (i p) c -> (s i) p c", p=P)[bass.ds(seq * NT + c * CT, CT), :, :]
                                     .rearrange("i p c -> p i c"), xt[:, c * CT:(c + 1) * CT, :]).then_inc(x_out, 16)
                    sp.wait_ge(x_out, 16 * NCH)
                    sp.wait_ge(w_in, 48)

                @block.tensor
                def _(pe):
                    def down(i):
                        pe.wait_ge(sq_done, NF * (i // CT + 1))
                        if i >= 2:
                            pe.wait_ge(y_ev, i - 1)
                        for j in range(NF):
                            mm = nc.tensor.matmul(bank(6 + i % 2)[:, 0:C], r2[i // CT][:, j, i % CT * P:(i % CT + 1) * P],
                                                  WpT[:, j, :], start=(j == 0), stop=(j == NF - 1))
                        mm.then_inc(y_mm, 1)

                    for s in range(NCH * NF):
                        c, j = s // NF, s % NF
                        if s >= 4:
                            pe.wait_ge(sq_done, s - 3)
                        for k in range(KC):
                            mm = nc.tensor.matmul(bank(s % 4), WfT[:, k, j * P:(j + 1) * P],
                                                  xnT[:, k, c * CH:(c + 1) * CH], start=(k == 0), stop=(k == KC - 1))
                        mm.then_inc(h_mm, 1)
                        for i in DOWN.get(s, ()):
                            down(i)

                @block.scalar
                def _(act):
                    for s in range(NCH * NF):
                        act.wait_ge(h_mm, s + 1)
                        if s >= 2:
                            act.wait_ge(sq_done, s - 1)
                        nc.scalar.activation(rl[:, s % 2, :], bank(s % 4), ACT.Relu).then_inc(relu_done, 1)
                        for i in DOWN.get(s, ()):
                            act.wait_ge(y_mm, i + 1)
                            nc.scalar.copy(ytok[:, i, :], bank(6 + i % 2)[:, 0:C]).then_inc(y_ev, 1)

                @block.vector
                def _(dve):
                    for s in range(NCH * NF):
                        dve.wait_ge(relu_done, s + 1)
                        nc.vector.tensor_tensor(r2[s // NF][:, s % NF, :], rl[:, s % 2, :], bank(s % 4), ALU.mult)\
                            .then_inc(sq_done, 1)
                    close_vector(dve, cs, 0, y_ev, last=True)

                @block.gpsimd
                def _(pool):
                    close_pool(pool, cs, 0, last=True)



def kernel(**inputs):
    import concourse.bacc as bacc
    from concourse.bass_utils import run_bass_kernel_spmd as run

    g = {k: np.asarray(v) for k, v in inputs.items()}

    def tiles(w):
        return w.reshape((-1, P) + w.shape[1:]).swapaxes(0, 1)

    def both(name, f):
        return np.stack([f(g[f"L1_attn_{d}_{name}"]) for d in ("fw", "bw")], axis=1)

    row = lambda w: w.reshape(1, -1)
    experts = lambda w: w.transpose(1, 0, 2).reshape(C, NE * HE)
    arrays = {
        "x": g["L0_attn_x"],
        "ident": np.eye(P, dtype=np.float32),
        "tri": np.broadcast_to(np.tril(np.ones((NE, NE), np.float32), -1).reshape(1, -1), (P, NE * NE)),
        "sel": (np.arange(NE)[:, None, None] == 2 * np.arange(NE // 2)[:, None] + np.arange(P) // HE)
        .astype(np.float32),
        "wqkT": tiles(np.concatenate([g["L0_attn_Wq"], g["L0_attn_Wk"]]).T),
        "wvT": tiles(g["L0_attn_Wv"].T), "woT": tiles(g["L0_attn_Wo"].T),
        "brow": row(np.concatenate([g["L0_attn_bq"], g["L0_attn_bk"], g["L0_attn_bv"]])), "bo": row(g["L0_attn_bo"]),
        "rwT": tiles(g["L0_ffn_router_w"].T), "cbias": row(g["L0_ffn_correction_bias"]),
        "wgT": tiles(np.concatenate([experts(g["L0_ffn_gate_w"]), g["L0_ffn_shared_gate_w"].T], axis=1)),
        "wuT": tiles(np.concatenate([experts(g["L0_ffn_up_w"]), g["L0_ffn_shared_up_w"].T], axis=1)),
        "wdn": tiles(np.concatenate([g["L0_ffn_down_w"].reshape(NE * HE, C), g["L0_ffn_shared_down_w"].T])),
        "inT": both("in_w", lambda w: tiles(w.T)),
        "xpT": both("xproj_w", lambda w: tiles(w.T)),
        "dtT": both("dt_w", lambda w: w.T),
        "convw": both("conv_w", lambda w: tiles(w[:, 0, :])),
        "convb": both("conv_b", tiles), "dtb": both("dt_b", tiles), "Dp": both("Dp", tiles),
        "alog": both("Alog", tiles),
        "outw": both("out_w", tiles),
        "projT": np.stack([tiles(g["L1_attn_proj_w"].T[i * C:(i + 1) * C]) for i in range(2)], axis=1),
        "projb": row(g["L1_attn_proj_b"]), "lnw": row(g["L1_attn_ln_w"]), "lnb": row(g["L1_attn_ln_b"]),
        "wfc": tiles(g["L1_ffn_w_fc"]), "wproj": tiles(g["L1_ffn_w_proj"]),
        "uT": g["L1_ffn_u"].T, "v": g["L1_ffn_v"], "fastb": g["L1_ffn_fast_b"],
        "gate": g["L1_ffn_gate"].reshape(1, 1),
    }
    nc = bacc.Bacc("TRN2", target_bir_lowering=False, num_devices=1)
    given, aps = {}, {}
    for name, w in arrays.items():
        w = np.ascontiguousarray(w)
        given[f"in_{name}"] = w
        aps[name] = nc.dram_tensor(f"in_{name}", w.shape, mybir.dt.from_np(w.dtype), kind="ExternalInput").ap()
    out = nc.dram_tensor("out_x", (NSEQ, T, C), F32, kind="ExternalOutput").ap()
    build(nc, aps, out)
    return run(nc, [given], core_ids=[0]).results[0]["out_x"]
```
